# Optimizing a Trainium2 kernel written in Bass

```python
import numpy as np
import jax
import jax.numpy as jnp

def _softmax(x, axis=-1):
    return jax.nn.softmax(x, axis=axis)

def _gelu(x):
    return jax.nn.gelu(x, approximate=True)

def _silu(x):
    return jax.nn.silu(x)

def _sigmoid(x):
    return jax.nn.sigmoid(x)

def _layernorm(x, axis=-1, eps=1e-05):
    m = jnp.mean(x, axis=axis, keepdims=True)
    v = jnp.var(x, axis=axis, keepdims=True)
    return (x - m) / jnp.sqrt(v + eps)

def _scatter_add(tgt, idx, src, axis=0):
    return tgt.at[idx].add(src)

def _segment_sum(src, seg, n):
    return jax.ops.segment_sum(src, seg, n)
kernel_name = 'mk_adj_resnorm_d1_adj_r2_68ea5c'

def setup_inputs(seed: int=0):
    np.random.seed(seed)
    _w = jnp.asarray

    def _rec_inputs():
        import jax
        import jax.numpy as jnp
        _gk = jax.random.key(seed)
        x = -0.0005207 + 1.001 * jax.random.normal(jax.random.fold_in(_gk, 1), (4096, 128), jnp.float32)
        _a = jax.random.bernoulli(jax.random.fold_in(_gk, 2), 0.000976562, (4096, 4096))
        _a = jnp.logical_or(_a, jnp.eye(4096, dtype=bool))
        _af = _a.astype(jnp.float32)
        adj = _af
        return (x, adj)
    x, adj = _rec_inputs()

    def _L0_gnn_setup():
        import jax, jax.numpy as jnp
        import numpy as np
        N = 4096
        D_IN = 128
        D_OUT = 128
        key = jax.random.key(seed)
        k_x, k_a, k_w, k_bias = jax.random.split(key, 4)
        x = jax.random.normal(k_x, (N, D_IN), dtype=jnp.float32)
        A_shape = jax.random.randint(k_a, (N, N), 0, 2).astype(jnp.float32)
        A_shape = A_shape.at[jnp.arange(N), jnp.arange(N)].set(1.0)
        lim = 1.0 / np.sqrt(D_IN)
        W = jax.random.uniform(k_w, (D_OUT, D_IN), jnp.float32, -lim, lim)
        bias = jax.random.uniform(k_bias, (D_OUT,), jnp.float32, -lim, lim)
        b = jnp.ones((1,), dtype=jnp.float32)
        return {'x': x, 'A_shape': A_shape, 'W': W, 'bias': bias, 'b': b}
    _L0_gnn_all = _L0_gnn_setup()
    _L0_gnn_in = {k: v for k, v in _L0_gnn_all.items() if k in ('W', 'bias', 'b')}
    del _L0_gnn_all
    return {'x': x, 'adj': adj, 'L0_gnn_W': _L0_gnn_in['W'], 'L0_gnn_bias': _L0_gnn_in['bias'], 'L0_gnn_b': _L0_gnn_in['b']}

def reference(x, adj, L0_gnn_W, L0_gnn_bias, L0_gnn_b):
    import jax
    import jax.numpy as jnp

    def _L0_gnn_ref(x, A_shape, W, bias, b):
        import jax, jax.numpy as jnp
        import numpy as np
        N = 4096
        D_IN = 128
        D_OUT = 128
        y = jnp.linalg.norm(x, axis=-1, keepdims=True)
        A = x @ x.T / (y @ y.T)
        A = A * b
        A = jnp.tanh(A / 8.0) * 8.0
        A = jnp.exp(A) * A_shape
        A = A / jnp.sum(A, axis=-1, keepdims=True)
        x = A @ x
        return x @ W.T + bias
    x = _layernorm(x + _L0_gnn_ref(x, adj, L0_gnn_W, L0_gnn_bias, L0_gnn_b), axis=-1)
    return x

_drawn_inputs = setup_inputs


def setup_inputs(seed=0):
    import zlib

    import numpy as np

    out = dict(_drawn_inputs(seed))
    spreads = {}
    factors = {}
    for name, (base, spread) in spreads.items():
        noise = np.random.default_rng([zlib.crc32(name.encode()), seed]).standard_normal(out[name].shape)
        drawn = base * np.exp(spread * noise) if base else spread * noise
        out[name] = jnp.asarray(drawn.astype(out[name].dtype))
    for name, factor in factors.items():
        out[name] = (out[name] * factor).astype(out[name].dtype)
    return out
```

```python
import concourse.bass as bass
from concourse import mybir
from contextlib import ExitStack



def adj_attention_layernorm(nc, x, adj, w, bias, b, out):
    fp32 = mybir.dt.float32
    fp16 = mybir.dt.float16
    ALU = mybir.AluOpType
    ACT = mybir.ActivationFunctionType
    AX = mybir.AxisListType

    N, D = x.shape
    P = 128
    Q = 32
    B = 512
    NB = N // B
    C = B // P
    NC = N // P
    F = D - 1
    SPLIT = 2.0 ** 12
    EPS = 1e-5
    NEAR = 3
    UNITS = 1 + NEAR
    FAR = NB // 2
    ABLK = 1 + 2 * NEAR
    RING = ABLK
    LOAD = 16 * (P // Q)

    ctx = ExitStack()
    with ctx:
        def sb(name, shape, dt=fp32):
            return ctx.enter_context(nc.sbuf_tensor(name, shape, dt))

        def pb(name, shape, dt=fp32):
            return ctx.enter_context(nc.psum_tensor(name, shape, dt))

        def sem(name):
            return ctx.enter_context(nc.semaphore(name))

        xrow = sb("xrow", [P, NC, D])
        xs = sb("xs", [P, NC, D])
        xhi = sb("xhi", [P, NC, P], fp16)
        xlo = sb("xlo", [P, NC, P], fp16)
        v = sb("v", [P, NC, D])
        acc = sb("acc", [P, N])
        raw = [sb(f"raw{s}", [P, B // Q, P]) for s in range(RING)]
        dT = [sb(f"dT{s}", [P, C, B]) for s in range(2)]
        xT = [sb(f"xT{s}", [P, C, B]) for s in range(2)]
        E = [sb(f"E{s}", [P, C, B]) for s in range(2)]
        vJ = [sb(f"vJ{s}", [P, C, D]) for s in range(2)]
        vI = sb("vI", [P, C, D])
        xsT = [sb(f"xsT{s}", [P, B]) for s in range(2)]
        ident = sb("ident", [P, P])
        restore = sb("restore", [P, D])
        wrow = sb("wrow", [P, P])
        wcT = sb("wcT", [P, P])
        wsum = sb("wsum", [P, 1])
        wmean = sb("wmean", [P, 1])
        nmean = sb("nmean", [P, NC])
        bcol = sb("bcol", [P, 1])
        scale = sb("scale", [P, 1])
        biasb = sb("biasb", [P, D])
        ssq = sb("ssq", [P, NC])
        root = sb("root", [P, NC])
        nrm = sb("nrm", [P, NC])
        quo = sb("quo", [P, NC])
        rn = sb("rn", [P, NC])
        vn = sb("vn", [P, NC])
        rs = sb("rs", [P, NC])
        y = [sb(f"y{s}", [P, C, D]) for s in range(2)]
        stat = sb("stat", [P, NC, 6])
        mv = sb("mv", [P, NC, 2])
        std = sb("std", [P, NC])
        rstd = sb("rstd", [P, NC])
        nmr = sb("nmr", [P, NC])
        epsc = sb("epsc", [P, 1])
        o = [sb(f"o{s}", [P, C, D]) for s in range(2)]
        sq = dT[0][:, :, :].rearrange("p c n -> p (c n)").rearrange("p (c n) -> p c n", n=D)

        S = pb("S", [P, C, B])
        ET = [pb(f"ET{s}", [P, B]) for s in range(2)]
        accD = pb("accD", [P, B])
        accX = pb("accX", [P, B])

        s_x = [sem(f"s_x{h}") for h in range(2)]
        s_w = sem("s_w")
        s_b = sem("s_b")
        s_bias = sem("s_bias")
        s_raw = [sem(f"s_raw{s}") for s in range(RING)]
        s_const = sem("s_const")
        s_id = sem("s_id")
        s_sq = sem("s_sq")
        s_ssq = sem("s_ssq")
        s_root = sem("s_root")
        s_nrm = sem("s_nrm")
        s_xs = sem("s_xs")
        s_wT = sem("s_wT")
        s_wc = sem("s_wc")
        s_xT = sem("s_xT")
        s_cpT = sem("s_cpT")
        s_hi = sem("s_hi")
        s_lo = sem("s_lo")
        s_z = sem("s_z")
        s_v = sem("s_v")
        s_S = sem("s_S")
        s_tanh = sem("s_tanh")
        s_E = sem("s_E")
        s_tr = sem("s_tr")
        s_ET = sem("s_ET")
        s_dmV = sem("s_dmV")
        s_dmP = sem("s_dmP")
        s_xm = sem("s_xm")
        s_dagg = sem("s_dagg")
        s_xagg = sem("s_xagg")
        s_addD = sem("s_addD")
        s_addX = sem("s_addX")
        s_vJ = [sem(f"s_vJ{s}") for s in range(2)]
        s_vI = sem("s_vI")
        s_xb = sem("s_xb")
        s_scale = sem("s_scale")
        s_mv1 = sem("s_mv1")
        s_sum = sem("s_sum")
        s_rs = sem("s_rs")
        s_fT = sem("s_fT")
        s_y = sem("s_y")
        s_yb = sem("s_yb")
        s_mv = sem("s_mv")
        s_bn = sem("s_bn")
        s_std = sem("s_std")
        s_nmr = sem("s_nmr")
        s_rstd = sem("s_rstd")
        s_o = sem("s_o")
        s_out = [sem(f"s_out{s}") for s in range(2)]

        block = ctx.enter_context(nc.Block())

        def bc(t, a, k, n):
            return t[:, a:a + k].unsqueeze(2).to_broadcast([P, k, n])

        ring_uses = [0] * RING
        far_raw = []
        for k in range(2 * FAR):
            ring_uses[(k - 1) % RING] += 1
            far_raw.append(((k - 1) % RING, LOAD * ring_uses[(k - 1) % RING], k))

        def far_unit(k):
            return dict(g=k, I=k, J=k + FAR, pair=True, pairs=k + 1, group=k, opens=True, closes=True, slot=k % 2, turn=k // 2,
                        raw=far_raw[2 * k:2 * k + 2], new_I=True, vI=k + 1, early=k < 2)

        def near_unit(I, u, J=None):
            first = 2 * u - 1 if u else 0
            return dict(g=FAR + UNITS * I + u, I=I, J=J if J is not None else (I + u) & (NB - 1) if u else I, pair=u > 0,
                        pairs=FAR + NEAR * I + u, group=FAR + I, opens=u == 0, closes=u == NEAR, slot=u % 2,
                        turn=FAR // 2 + UNITS // 2 * I + u // 2,
                        raw=[(s, (I + ring_uses[s] + 1) * LOAD, 2 * FAR + ABLK * I + s)
                             for s in range(first, first + (2 if u else 1))],
                        new_I=u == 1, vI=FAR + I + 1, early=False)

        straight = [far_unit(k) for k in range(FAR)] + [near_unit(0, u) for u in range(UNITS)]
        last = [near_unit(NB - 1, u) for u in range(UNITS)]

        def run(engine, step):
            for k, t in enumerate(straight):
                step(t, straight[k - 1] if k >= 1 else None, straight[k - 2] if k >= 2 else None)
            J_regs = [engine.alloc_register(f"J{u}") for u in range(1, UNITS)]
            with engine.Fori(1, NB) as I:
                J = [I]
                for u in range(1, UNITS):
                    engine.reg_alu(J_regs[u - 1], I, u, ALU.add)
                    engine.reg_alu(J_regs[u - 1], J_regs[u - 1], NB - 1, ALU.bitwise_and)
                    J.append(engine.snap(J_regs[u - 1], min_val=0, max_val=NB - 1))
                line = [near_unit(I - 1, UNITS - 2), near_unit(I - 1, UNITS - 1)] + \
                       [near_unit(I, u, J[u]) for u in range(UNITS)]
                for k in range(2, len(line)):
                    step(line[k], line[k - 1], line[k - 2])

        @block.sync
        def _(sp):
            for J in range(NB):
                for q in range(P // Q):
                    src = x[J * B + P * q:J * B + P * q + P, :].rearrange("(c r) d -> r c d", r=Q)
                    sp.dma_start(xrow[Q * q:Q * q + Q, C * J:C * J + C, :], src).then_inc(s_x[2 * J // NB], 16)

            def load(place, rows, cols):
                slot, _, before = place
                if not isinstance(before, int) or before >= RING:
                    sp.wait_ge(s_tr, before - RING + 1)
                for q in range(P // Q):
                    src = adj[bass.ds(rows * B, B), bass.ds(cols * B + P * q, P)]
                    sp.dma_start(raw[slot][Q * q:Q * q + Q, :, :], src.rearrange("(i r) n -> r i n", r=Q)) \
                        .then_inc(s_raw[slot], 16)

            def step(t, p1, p2):
                load(t["raw"][0], t["I"], t["J"])
                if t["pair"]:
                    load(t["raw"][1], t["J"], t["I"])
            run(sp, step)
            for J in range(NB):
                sp.wait_ge(s_o, J + 1)
                for q in range(P // Q):
                    dst = out[J * B + P * q:J * B + P * q + P, :].rearrange("(c r) d -> r c d", r=Q)
                    sp.dma_start(dst, o[J % 2][Q * q:Q * q + Q, :, :]).then_inc(s_out[J % 2], 16)
            for s in range(2):
                sp.wait_ge(s_out[s], LOAD * (NB // 2))

        @block.gpsimd
        def _(pool):
            nc.gpsimd.memset(ident[:, :], 0.0).then_inc(s_id, 1)
            nc.gpsimd.memset(restore[:, :], 0.0).then_inc(s_id, 1)
            pool.wait_ge(s_id, 2)
            for m in (ident, restore):
                nc.gpsimd.affine_select(out=m[:, :], in_=m[:, :], compare_op=ALU.not_equal, fill=1.0, base=0,
                                        pattern=[[-1, P]], channel_multiplier=1).then_inc(s_id, 1)
            pool.wait_ge(s_id, 4)
            nc.gpsimd.memset(restore[:, F:D], -1.0).then_inc(s_id, 1)
            pool.wait_ge(s_id, 5)
            nc.gpsimd.affine_select(out=restore[:, F:D], in_=restore[:, F:D], compare_op=ALU.not_equal, fill=0.0,
                                    base=-F, pattern=[[0, 1]], channel_multiplier=1).then_inc(s_id, 1)
            nc.gpsimd.memset(v[:, :, F:D], 1.0).then_inc(s_const, 1)
            nc.gpsimd.memset(acc[:, :], 0.0).then_inc(s_const, 1)
            nc.gpsimd.memset(epsc[:, :], EPS).then_inc(s_const, 1)
            pool.wait_ge(s_const, 3)

            def step(t, p1, p2):
                if t["opens"] and not t["pair"]:
                    if t is straight[FAR]:
                        pool.wait_ge(s_bias, 16)
                    part = xrow[:, bass.ds(t["I"] * C, C), :]
                    nc.gpsimd.tensor_tensor(part, part, biasb[:, :].unsqueeze(1).to_broadcast([P, C, D]), ALU.add) \
                        .then_inc(s_xb, 1)
                pool.wait_ge(s_tr, t["raw"][0][2] + 1)
                pool.wait_ge(s_E, t["g"] * 2 + 2)
                for c in range(C // 2, C):
                    nc.gpsimd.tensor_tensor(dT[t["slot"]][:, c, :], E[t["slot"]][:, c, :], dT[t["slot"]][:, c, :],
                                            ALU.mult).then_inc(s_dmP, 1)

            run(pool, step)

        @block.scalar
        def _(act):
            act.dma_start(wrow[:, :], w[:, :]).then_inc(s_w, 16)
            act.dma_start(bcol[:, :], b.rearrange("(o n) -> o n", o=1).to_broadcast([P, 1])).then_inc(s_b, 16)
            act.dma_start(biasb[:, :], bias.rearrange("(o n) -> o n", o=1).to_broadcast([P, D])).then_inc(s_bias, 16)
            act.wait_ge(s_b, 16)
            nc.scalar.activation(scale[:, :], bcol[:, :], ACT.Copy, scale=1.0 / (8.0 * SPLIT * SPLIT)) \
                .then_inc(s_scale, 1)
            H = NC // 2
            for h in range(2):
                act.wait_ge(s_x[h], 16 * (NB // 2) * (P // Q))
                if h:
                    act.wait_ge(s_ssq, 1)
                nc.scalar.activation(sq, xrow[:, H * h:H * h + H, :], ACT.Square).then_inc(s_sq, 1)
            act.wait_ge(s_ssq, 2)
            nc.scalar.activation(root[:, :], ssq[:, :], ACT.Sqrt).then_inc(s_root, 1)
            for J in range(NB):
                act.wait_ge(s_xT, J + 1)
                nc.scalar.activation(xhi[:, C * J:C * J + C, :].rearrange("p c n -> p (c n)"), ET[J % 2][:, :],
                                     ACT.Copy).then_inc(s_hi, 1)
                if J >= 2:
                    act.wait_ge(s_z, J - 1)
                nc.scalar.activation(xsT[J % 2][:, :], ET[J % 2][:, :], ACT.Copy).then_inc(s_cpT, 1)
            act.wait_ge(s_scale, 1)
            act.wait_ge(s_v, NB)
            act.wait_ge(s_const, 3)

            def copy_v(dst, blk, s_done):
                act.dma_start(dst[:, :, :], v[:, bass.ds(blk * C, C), :]).then_inc(s_done, 16)

            def step(t, p1, p2):
                if p1 is not None and p1["new_I"]:
                    if not isinstance(p1["pairs"], int) or p1["pairs"] > 1:
                        act.wait_ge(s_xagg, p1["pairs"] - 1)
                    copy_v(vI, p1["I"], s_vI)
                if not t["early"]:
                    act.wait_ge(s_dagg, p2["g"] + 1)
                copy_v(vJ[t["slot"]], t["J"], s_vJ[t["slot"]])
                for h in range(2):
                    half = S[:, 2 * h:2 * h + 2, :]
                    act.wait_ge(s_S, t["g"] * 2 + (h + 1))
                    nc.scalar.activation(half, half, ACT.Tanh, scale=scale[:, :]).then_inc(s_tanh, 1)
                    if h == 0 and not t["early"]:
                        act.wait_ge(s_dmV, p2["g"] * 2 + 2)
                        act.wait_ge(s_dmP, p2["g"] * 2 + 2)
                        act.wait_ge(s_ET, p2["pairs"] * C)
                    act.wait_ge(s_tanh, t["g"] * 2 + (h + 1))
                    nc.scalar.activation(E[t["slot"]][:, 2 * h:2 * h + 2, :], half, ACT.Exp, scale=8.0) \
                        .then_inc(s_E, 1)

            run(act, step)
            for J in range(NB):
                act.wait_ge(s_mv, J + 1)
                nc.scalar.activation(std[:, C * J:C * J + C], mv[:, C * J:C * J + C, 1], ACT.Sqrt,
                                     bias=epsc[:, :]).then_inc(s_std, 1)
                act.wait_ge(s_nmr, J + 1)
                if J >= 2:
                    act.wait_ge(s_out[J % 2], LOAD * (J // 2))
                for c in range(C):
                    k = C * J + c
                    done = nc.scalar.activation(o[J % 2][:, c, :], y[J % 2][:, c, :], ACT.Identity,
                                                scale=rstd[:, k:k + 1], bias=nmr[:, k:k + 1])
                done.then_inc(s_o, 1)

        @block.vector
        def _(dve):
            H = NC // 2
            for h in range(2):
                dve.wait_ge(s_sq, h + 1)
                nc.vector.tensor_reduce(ssq[:, H * h:H * h + H], sq, axis=AX.X, op=ALU.add).then_inc(s_ssq, 1)
            dve.wait_ge(s_root, 1)
            nc.vector.reciprocal(quo[:, :], root[:, :]).then_inc(s_nrm, 1)
            dve.wait_ge(s_nrm, 1)
            nc.vector.tensor_tensor(quo[:, :], quo[:, :], ssq[:, :], ALU.mult).then_inc(s_nrm, 1)
            dve.wait_ge(s_nrm, 2)
            nc.vector.tensor_tensor(quo[:, :], quo[:, :], root[:, :], ALU.add).then_inc(s_nrm, 1)
            dve.wait_ge(s_nrm, 3)
            nc.vector.tensor_scalar(vn[:, :], quo[:, :], 0.5 / SPLIT, None, ALU.mult).then_inc(s_nrm, 1)
            dve.wait_ge(s_nrm, 4)
            nc.vector.reciprocal(rn[:, :], vn[:, :]).then_inc(s_nrm, 1)
            dve.wait_ge(s_nrm, 5)
            for J in range(NB):
                nc.vector.tensor_tensor(xs[:, C * J:C * J + C, :], xrow[:, C * J:C * J + C, :], bc(rn, C * J, C, D),
                                        ALU.mult).then_inc(s_xs, 1)
            dve.wait_ge(s_wT, 1)
            nc.vector.tensor_reduce(wsum[:, :], accD[:, 0:P], axis=AX.X, op=ALU.add).then_inc(s_wc, 1)
            dve.wait_ge(s_wc, 1)
            nc.vector.tensor_scalar(wmean[:, :], wsum[:, :], 1.0 / D, None, ALU.mult).then_inc(s_wc, 1)
            dve.wait_ge(s_wc, 2)
            nc.vector.tensor_scalar(wcT[:, :], accD[:, 0:P], wmean[:, 0:1], None, ALU.subtract).then_inc(s_wc, 1)
            for J in range(NB):
                rows = slice(C * J, C * J + C)
                dve.wait_ge(s_cpT, J + 1)
                nc.vector.tensor_tensor(xlo[:, rows, :].rearrange("p c n -> p (c n)"), ET[J % 2][:, :],
                                        xhi[:, rows, :].rearrange("p c n -> p (c n)"), ALU.subtract) \
                    .then_inc(s_lo, 1)
                dve.wait_ge(s_z, J + 1)
                nc.vector.tensor_tensor(v[:, rows, 0:F], S[:, J % 2, :].rearrange("p (c n) -> p c n", n=D)[:, :, 0:F],
                                        bc(vn, C * J, C, F), ALU.mult).then_inc(s_v, 1)
            dve.wait_ge(s_const, 3)

            def transposes(place, dst):
                slot, arrived, _ = place
                dve.wait_ge(s_raw[slot], arrived)
                nc.vector.transpose(dst[:, :, :].rearrange("p c (k q r) -> p c q k r", q=P // Q, r=Q),
                                    raw[slot][:, :, :].rearrange("p i (c r) -> p c i r", r=Q)).then_inc(s_tr, 1)

            def add(total, rows, done):
                part = acc[:, bass.ds(rows * B, B)]
                nc.vector.tensor_tensor(part, total[:, :], part, ALU.add).then_inc(done, 1)

            def adds(p):
                if p["pair"]:
                    dve.wait_ge(s_xagg, p["pairs"])
                    if not isinstance(p["pairs"], int) or p["pairs"] > 1:
                        dve.wait_ge(s_addX, p["pairs"] - 1)
                        dve.wait_ge(s_addD, p["group"])
                    add(accX, p["J"], s_addX)
                if p["closes"]:
                    dve.wait_ge(s_dagg, p["g"] + 1)
                    dve.wait_ge(s_addX, p["pairs"])
                    if not isinstance(p["group"], int) or p["group"] > 0:
                        dve.wait_ge(s_addD, p["group"])
                    add(accD, p["I"], s_addD)

            def step(t, p1, p2):
                s = t["slot"]
                if not t["early"]:
                    dve.wait_ge(s_dagg, p2["g"] + 1)
                transposes(t["raw"][0], dT[s])
                if p2 is not None:
                    adds(p2)
                if t["pair"]:
                    if not t["early"]:
                        dve.wait_ge(s_xagg, p2["pairs"])
                    transposes(t["raw"][1], xT[s])
                dve.wait_ge(s_E, t["g"] * 2 + 1)
                dve.wait_ge(s_tr, t["raw"][-1][2] + 1)
                for c in range(C // 2):
                    nc.vector.tensor_tensor(dT[s][:, c, :], E[s][:, c, :], dT[s][:, c, :], ALU.mult) \
                        .then_inc(s_dmV, 1)
                if t["pair"]:
                    for c in range(C):
                        dve.wait_ge(s_ET, (t["pairs"] - 1) * C + (c + 1))
                        nc.vector.tensor_tensor(xT[s][:, c, :], ET[c % 2][:, :], xT[s][:, c, :], ALU.mult) \
                            .then_inc(s_xm, 1)

            run(dve, step)
            adds(last[-2])
            adds(last[-1])
            dve.wait_ge(s_sum, 1)
            nc.vector.reciprocal(rs[:, :], accX[:, 0:NC]).then_inc(s_rs, 1)
            dve.wait_ge(s_rs, 1)
            dve.wait_ge(s_xb, NB)
            for J in range(NB):
                rows = slice(C * J, C * J + C)
                dve.wait_ge(s_fT, J + 1)
                if J >= 2:
                    dve.wait_ge(s_o, J - 1)
                nc.vector.tensor_tensor(y[J % 2][:, :, :], S[:, J % C, :].rearrange("p (c n) -> p c n", n=D),
                                        bc(rs, C * J, C, D), ALU.mult).then_inc(s_y, 1)
                dve.wait_ge(s_y, J + 1)
                nc.vector.tensor_tensor(y[J % 2][:, :, :], y[J % 2][:, :, :], xrow[:, rows, :], ALU.add) \
                    .then_inc(s_yb, 1)
                dve.wait_ge(s_yb, J + 1)
                for k in range(C * J, C * J + C):
                    nc.vector.bn_stats(stat[:, k, :], y[J % 2][:, k - C * J, :]).then_inc(s_bn, 1)
                dve.wait_ge(s_bn, C * J + C)
                for k in range(C * J, C * J + C):
                    done = nc.vector.bn_aggr(mv[:, k, :], stat[:, k, :])
                    done.then_inc(s_mv1, 1)
                dve.wait_ge(s_mv1, C * J + C)
                nc.vector.tensor_scalar(nmean[:, rows], mv[:, rows, 0], -1.0, None, ALU.mult).then_inc(s_mv, 1)
                dve.wait_ge(s_std, J + 1)
                nc.vector.reciprocal(rstd[:, rows], std[:, rows]).then_inc(s_rstd, 1)
                dve.wait_ge(s_rstd, J + 1)
                dve.wait_ge(s_mv, J + 1)
                nc.vector.tensor_tensor(nmr[:, rows], nmean[:, rows], rstd[:, rows], ALU.mult).then_inc(s_nmr, 1)

        @block.tensor
        def _(pe):
            pe.wait_ge(s_id, 6)
            pe.wait_ge(s_w, 16)
            nc.tensor.transpose(accD[:, 0:P], wrow[:, :], ident[:, :]).then_inc(s_wT, 1)
            for J in range(NB + 1):
                if J < NB:
                    pe.wait_ge(s_xs, J + 1)
                    if J >= 2:
                        pe.wait_ge(s_cpT, J - 1)
                        pe.wait_ge(s_lo, J - 1)
                    for c in range(C):
                        done = nc.tensor.transpose(ET[J % 2][:, P * c:P * c + P], xs[:, C * J + c, :], ident[:, :])
                    done.then_inc(s_xT, 1)
                if J >= 1:
                    K = J - 1
                    if K == 0:
                        pe.wait_ge(s_wc, 3)
                    pe.wait_ge(s_cpT, K + 1)
                    if K >= 2:
                        pe.wait_ge(s_v, K - 1)
                    for c in range(C):
                        done = nc.tensor.matmul(S[:, K % 2, P * c:P * c + P], xsT[K % 2][:, P * c:P * c + P],
                                                wcT[:, :], start=True, stop=True)
                    done.then_inc(s_z, 1)
            pe.wait_ge(s_lo, NB)
            pe.wait_ge(s_v, NB)

            def moving(part, blk):
                return part[:, bass.ds(blk * C, C), :].rearrange("p c n -> p (c n)")

            def cosines(t):
                for c in range(C):
                    if not (isinstance(t["g"], int) and t["g"] == 0) and c % 2 == 0:
                        pe.wait_ge(s_E, t["g"] * 2 - 1 + c // 2)
                    for k, (left, right) in enumerate(((xhi, xhi), (xhi, xlo), (xlo, xhi))):
                        done = nc.tensor.matmul(S[:, c, :], left[:, t["J"] * C + c, :], moving(right, t["I"]),
                                                start=k == 0, stop=k == 2)
                    if c % 2:
                        done.then_inc(s_S, 1)

            def aggregate_d(p):
                pe.wait_ge(s_vJ[p["slot"]], (p["turn"] + 1) * 16)
                if p["opens"] and not (isinstance(p["group"], int) and p["group"] == 0):
                    pe.wait_ge(s_addD, p["group"])
                for c in range(C):
                    if c == 0:
                        pe.wait_ge(s_dmV, p["g"] * 2 + 2)
                    if c == C // 2:
                        pe.wait_ge(s_dmP, p["g"] * 2 + 2)
                    done = nc.tensor.matmul(accD[:, :], vJ[p["slot"]][:, c, :], dT[p["slot"]][:, c, :],
                                            start=p["opens"] and c == 0, stop=p["closes"] and c == C - 1)
                done.then_inc(s_dagg, 1)

            def aggregate_x(p, h):
                if h == 0:
                    pe.wait_ge(s_vI, p["vI"] * 16)
                    if not isinstance(p["pairs"], int) or p["pairs"] > 1:
                        pe.wait_ge(s_addX, p["pairs"] - 1)
                    pe.wait_ge(s_xm, p["pairs"] * C)
                for c in range(2 * h, 2 * h + 2):
                    done = nc.tensor.matmul(accX[:, :], vI[:, c, :], xT[p["slot"]][:, c, :],
                                            start=c == 0, stop=c == C - 1)
                if h == 1:
                    done.then_inc(s_xagg, 1)

            def transpose_E(t, h):
                pe.wait_ge(s_E, t["g"] * 2 + 2)
                for k in range(2 * h, 2 * h + 2):
                    if k < 2:
                        if isinstance(t["pairs"], int) and t["pairs"] == 1:
                            pass
                        else:
                            pe.wait_ge(s_xm, (t["pairs"] - 1) * C - (1 - k))
                    else:
                        pe.wait_ge(s_xm, (t["pairs"] - 1) * C + (k - 1))
                    for c in range(C):
                        done = nc.tensor.transpose(ET[k % 2][:, P * c:P * c + P],
                                                   E[t["slot"]][:, c, P * k:P * k + P], ident[:, :])
                    done.then_inc(s_ET, 1)

            def step(t, p1, p2):
                cosines(t)
                if p1 is not None:
                    aggregate_d(p1)
                for h in range(2):
                    if t["pair"]:
                        transpose_E(t, h)
                    if p1 is not None and p1["pair"]:
                        aggregate_x(p1, h)

            run(pe, step)
            aggregate_d(last[-1])
            aggregate_x(last[-1], 0)
            aggregate_x(last[-1], 1)
            pe.wait_ge(s_addX, last[-1]["pairs"])
            pe.wait_ge(s_addD, last[-1]["group"] + 1)
            for k in range(NC):
                done = nc.tensor.matmul(accX[:, k:k + 1], acc[:, P * k:P * k + P], ident[:, F:D], start=True, stop=True)
            done.then_inc(s_sum, 1)
            for J in range(NB):
                if J >= C:
                    pe.wait_ge(s_y, J - C + 1)
                for c in range(C):
                    k = C * J + c
                    done = nc.tensor.matmul(S[:, J % C, P * c:P * c + P], acc[:, P * k:P * k + P], restore[:, :],
                                            start=True, stop=True)
                done.then_inc(s_fT, 1)


def kernel(x, adj, L0_gnn_W, L0_gnn_bias, L0_gnn_b):
    import numpy as np
    import concourse.bacc as bacc
    from concourse.bass_utils import run_bass_kernel_spmd

    nc = bacc.Bacc("TRN2", target_bir_lowering=False, num_devices=1)
    arrays = dict(x=x, adj=adj, w=L0_gnn_W, bias=L0_gnn_bias, b=L0_gnn_b)
    arrays = {f"in_{k}": np.ascontiguousarray(a) for k, a in arrays.items()}
    ins = [nc.dram_tensor(k, a.shape, mybir.dt.from_np(a.dtype), kind="ExternalInput").ap() for k, a in arrays.items()]
    out = nc.dram_tensor("out", x.shape, mybir.dt.float32, kind="ExternalOutput").ap()
    adj_attention_layernorm(nc, *ins, out)
    return run_bass_kernel_spmd(nc, [arrays], core_ids=[0]).results[0]["out"]
```

```python
import concourse.bass as bass
from concourse import mybir
from contextlib import ExitStack



def adj_attention_layernorm(nc, x, adj, w, bias, b, out):
    fp32 = mybir.dt.float32
    fp16 = mybir.dt.float16
    ALU = mybir.AluOpType
    ACT = mybir.ActivationFunctionType
    AX = mybir.AxisListType

    N, D = x.shape
    P = 128
    Q = 32
    B = 512
    NB = N // B
    C = B // P
    NC = N // P
    F = D - 1
    SPLIT = 2.0 ** 12
    EPS = 1e-5
    NEAR = 3
    UNITS = 1 + NEAR
    FAR = NB // 2
    ABLK = 1 + 2 * NEAR
    RING = ABLK
    LOAD = 16 * (P // Q)

    ctx = ExitStack()
    with ctx:
        def sb(name, shape, dt=fp32):
            return ctx.enter_context(nc.sbuf_tensor(name, shape, dt))

        def pb(name, shape, dt=fp32):
            return ctx.enter_context(nc.psum_tensor(name, shape, dt))

        def sem(name):
            return ctx.enter_context(nc.semaphore(name))

        xrow = sb("xrow", [P, NC, D])
        xs = sb("xs", [P, NC, D])
        xhi = sb("xhi", [P, NC, P], fp16)
        xlo = sb("xlo", [P, NC, P], fp16)
        v = sb("v", [P, NC, D])
        acc = sb("acc", [P, N])
        raw = [sb(f"raw{s}", [P, B // Q, P]) for s in range(RING)]
        dT = [sb(f"dT{s}", [P, C, B]) for s in range(2)]
        xT = [sb(f"xT{s}", [P, C, B]) for s in range(2)]
        E = [sb(f"E{s}", [P, C, B]) for s in range(2)]
        vJ = [sb(f"vJ{s}", [P, C, D]) for s in range(2)]
        vI = sb("vI", [P, C, D])
        xsT = [sb(f"xsT{s}", [P, B]) for s in range(2)]
        ident = sb("ident", [P, P])
        restore = sb("restore", [P, D + 1])
        wrow = sb("wrow", [P, P])
        wcT = sb("wcT", [P, P])
        wsum = sb("wsum", [P, 1])
        wmean = sb("wmean", [P, 1])
        bcol = sb("bcol", [P, 1])
        scale = sb("scale", [P, 1])
        biasb = sb("biasb", [P, D])
        ssq = sb("ssq", [P, NC])
        root = sb("root", [P, NC])
        nrm = sb("nrm", [P, NC])
        quo = sb("quo", [P, NC])
        rn = sb("rn", [P, NC])
        vn = sb("vn", [P, NC])
        rs = sb("rs", [P, NC])
        var = sb("var", [P, NC])
        std = sb("std", [P, NC])
        rstd = sb("rstd", [P, NC])
        xmean = sb("xmean", [P, NC])
        epsc = sb("epsc", [P, 1])
        o = [xs[:, C * s:C * s + C, :] for s in range(4)]
        y = [xs[:, C * s:C * s + C, :] for s in range(4, 8)]
        squares = [t[:, :, :].rearrange("p c n -> p (c n)").rearrange("p (j c n) -> p j c n", c=C, n=D)
                   for t in (dT[0], dT[1])]
        junk = sb("junk", [P, C, D])

        S = pb("S", [P, C, B])
        ET = [pb(f"ET{s}", [P, B]) for s in range(2)]
        accD = pb("accD", [P, B])
        accX = pb("accX", [P, B])

        s_x = [sem(f"s_x{h}") for h in range(2)]
        s_raw = [sem(f"s_raw{s}") for s in range(RING)]
        s_vJ = [sem(f"s_vJ{s}") for s in range(2)]
        s_out = [sem(f"s_out{s}") for s in range(4)]
        s_w = sem("s_w")
        s_b = sem("s_b")
        s_bias = sem("s_bias")
        s_const = sem("s_const")
        s_id = sem("s_id")
        s_sq = sem("s_sq")
        s_ssq = sem("s_ssq")
        s_root = sem("s_root")
        s_nrm = sem("s_nrm")
        s_xs = sem("s_xs")
        s_wT = sem("s_wT")
        s_wc = sem("s_wc")
        s_xT = sem("s_xT")
        s_hi = sem("s_hi")
        s_cpT = sem("s_cpT")
        s_loV = sem("s_loV")
        s_loP = sem("s_loP")
        s_z = sem("s_z")
        s_v = sem("s_v")
        s_S = sem("s_S")
        s_tanh = sem("s_tanh")
        s_E = sem("s_E")
        s_tr = sem("s_tr")
        s_ET = sem("s_ET")
        s_dmV = sem("s_dmV")
        s_dmP = sem("s_dmP")
        s_xm = sem("s_xm")
        s_dagg = sem("s_dagg")
        s_xagg = sem("s_xagg")
        s_addD = sem("s_addD")
        s_addX = sem("s_addX")
        s_vI = sem("s_vI")
        s_scale = sem("s_scale")
        s_xb = sem("s_xb")
        s_xmean = sem("s_xmean")
        s_xc = sem("s_xc")
        s_fT = sem("s_fT")
        s_rs = sem("s_rs")
        s_y = sem("s_y")
        s_ssy = sem("s_ssy")
        s_std = sem("s_std")
        s_rstd = sem("s_rstd")
        s_o = sem("s_o")

        block = ctx.enter_context(nc.Block())

        def block_of(J):
            return slice(C * J, C * J + C)

        def bc(t, J, n):
            return t[:, block_of(J)].unsqueeze(2).to_broadcast([P, C, n])

        def pairs_of(t, first, last):
            return t[:, :].rearrange("p (h j c) -> p h j c", h=2, c=C)[:, :, first:last, :]

        ring_uses = [0] * RING
        far_raw = []
        for k in range(2 * FAR):
            ring_uses[(k - 1) % RING] += 1
            far_raw.append(((k - 1) % RING, LOAD * ring_uses[(k - 1) % RING], k))

        def far_unit(k):
            return dict(g=k, I=k, J=k + FAR, pair=True, pairs=k + 1, group=k, opens=True, closes=True, slot=k % 2, turn=k // 2,
                        raw=far_raw[2 * k:2 * k + 2], new_I=True, vI=k + 1, early=k < 2)

        def near_unit(I, u, J=None):
            first = 2 * u - 1 if u else 0
            return dict(g=FAR + UNITS * I + u, I=I, J=J if J is not None else (I + u) & (NB - 1) if u else I, pair=u > 0,
                        pairs=FAR + NEAR * I + u, group=FAR + I, opens=u == 0, closes=u == NEAR, slot=u % 2,
                        turn=FAR // 2 + UNITS // 2 * I + u // 2,
                        raw=[(s, (I + ring_uses[s] + 1) * LOAD, 2 * FAR + ABLK * I + s)
                             for s in range(first, first + (2 if u else 1))],
                        new_I=u == 1, vI=FAR + I + 1, early=False)

        straight = [far_unit(k) for k in range(FAR)] + [near_unit(0, u) for u in range(UNITS)]
        last = [near_unit(NB - 1, u) for u in range(UNITS)]

        def place_of(t):
            return t["g"] if isinstance(t["g"], int) else None

        def final_of(J):
            two = S[:, 2 * (J % 2):2 * (J % 2) + 2, 0:2 * (D + 2)]
            return two.rearrange("p a (c n) -> p a c n", c=2)

        x_pairs = xrow[:, :, :].rearrange("p (h j c) d -> p h j c d", h=2, c=C)

        def run(engine, step):
            for k, t in enumerate(straight):
                step(t, straight[k - 1] if k >= 1 else None, straight[k - 2] if k >= 2 else None)
            J_regs = [engine.alloc_register(f"J{u}") for u in range(1, UNITS)]
            with engine.Fori(1, NB) as I:
                J = [I]
                for u in range(1, UNITS):
                    engine.reg_alu(J_regs[u - 1], I, u, ALU.add)
                    engine.reg_alu(J_regs[u - 1], J_regs[u - 1], NB - 1, ALU.bitwise_and)
                    J.append(engine.snap(J_regs[u - 1], min_val=0, max_val=NB - 1))
                line = [near_unit(I - 1, UNITS - 2), near_unit(I - 1, UNITS - 1)] + \
                       [near_unit(I, u, J[u]) for u in range(UNITS)]
                for k in range(2, len(line)):
                    step(line[k], line[k - 1], line[k - 2])

        def load_x(engine, half):
            for q in range(2 * half, 2 * half + 2):
                for c in range(C):
                    src = x.rearrange("(j q c r) d -> q c r j d", q=P // Q, c=C, r=Q)[q, c]
                    dst = xrow[Q * q:Q * q + Q, :, :].rearrange("p (j c) d -> p j c d", c=C)[:, :, c, :]
                    engine.dma_start(dst, src).then_inc(s_x[half], 16)

        @block.sync
        def _(sp):
            load_x(sp, 0)

            def load(place, rows, cols):
                slot, _, before = place
                if not isinstance(before, int) or before >= RING:
                    sp.wait_ge(s_tr, before - RING + 1)
                for q in range(P // Q):
                    src = adj[bass.ds(rows * B, B), bass.ds(cols * B + P * q, P)]
                    sp.dma_start(raw[slot][Q * q:Q * q + Q, :, :], src.rearrange("(i r) n -> r i n", r=Q)) \
                        .then_inc(s_raw[slot], 16)

            def step(t, p1, p2):
                load(t["raw"][0], t["I"], t["J"])
                if t["pair"]:
                    load(t["raw"][1], t["J"], t["I"])
            run(sp, step)
            for J in range(NB):
                sp.wait_ge(s_o, J + 1)
                for q in range(P // Q):
                    dst = out[J * B + P * q:J * B + P * q + P, :].rearrange("(c r) d -> r c d", r=Q)
                    sp.dma_start(dst, o[J % 4][Q * q:Q * q + Q, :, :]).then_inc(s_out[J % 4], 16)
            for s in range(4):
                sp.wait_ge(s_out[s], LOAD * (NB // 4))

        @block.gpsimd
        def _(pool):
            load_x(pool, 1)
            nc.gpsimd.memset(ident[:, :], 0.0).then_inc(s_id, 1)
            nc.gpsimd.memset(restore[:, :], 0.0).then_inc(s_id, 1)
            pool.wait_ge(s_id, 2)
            nc.gpsimd.affine_select(out=ident[:, :], in_=ident[:, :], compare_op=ALU.not_equal, fill=1.0, base=0,
                                    pattern=[[-1, P]], channel_multiplier=1).then_inc(s_id, 1)
            nc.gpsimd.affine_select(out=restore[:, 0:F], in_=restore[:, 0:F], compare_op=ALU.not_equal, fill=1.0,
                                    base=0, pattern=[[-1, F]], channel_multiplier=1).then_inc(s_id, 1)
            nc.gpsimd.memset(restore[:, F:D], -1.0).then_inc(s_id, 1)
            pool.wait_ge(s_id, 5)
            nc.gpsimd.affine_select(out=restore[:, F:D], in_=restore[:, F:D], compare_op=ALU.not_equal, fill=0.0,
                                    base=-F, pattern=[[0, 1]], channel_multiplier=1).then_inc(s_id, 1)
            nc.gpsimd.affine_select(out=restore[:, D:D + 1], in_=restore[:, D:D + 1], compare_op=ALU.not_equal,
                                    fill=1.0, base=-F, pattern=[[0, 1]], channel_multiplier=1).then_inc(s_id, 1)
            nc.gpsimd.memset(v[:, :, F:D], 1.0).then_inc(s_const, 1)
            nc.gpsimd.memset(acc[:, :], 0.0).then_inc(s_const, 1)
            nc.gpsimd.memset(epsc[:, :], EPS).then_inc(s_const, 1)

            def lower_part(k):
                pool.wait_ge(s_cpT, 2 * k + 2)
                rows = block_of(k + FAR)
                nc.gpsimd.tensor_tensor(xlo[:, rows, :].rearrange("p c n -> p (c n)"), xsT[1][:, :],
                                        xhi[:, rows, :].rearrange("p c n -> p (c n)"), ALU.subtract) \
                    .then_inc(s_loP, 1)

            lower_part(0)

            def step(t, p1, p2):
                pool.wait_ge(s_tr, t["raw"][0][2] + 1)
                pool.wait_ge(s_E, t["g"] * 2 + 2)
                for c in range(C // 2, C):
                    nc.gpsimd.tensor_tensor(dT[t["slot"]][:, c, :], E[t["slot"]][:, c, :], dT[t["slot"]][:, c, :],
                                            ALU.mult).then_inc(s_dmP, 1)
                k = place_of(t)
                if k is not None and k < FAR:
                    if k + 1 < FAR:
                        lower_part(k + 1)
                    if k == 0:
                        pool.wait_ge(s_xs, NB)
                        pool.wait_ge(s_bias, 16)
                    for J in (2 * k, 2 * k + 1):
                        part = xrow[:, block_of(J), :]
                        nc.gpsimd.tensor_tensor(part, part, biasb[:, :].unsqueeze(1).to_broadcast([P, C, D]),
                                                ALU.add).then_inc(s_xb, 1)
                elif k is not None:
                    for J in (2 * (k - FAR), 2 * (k - FAR) + 1):
                        pool.wait_ge(s_xmean, J + 1)
                        part = xrow[:, block_of(J), :]
                        nc.gpsimd.tensor_tensor(part, part, bc(xmean, J, D), ALU.subtract).then_inc(s_xc, 1)

            run(pool, step)
            for J in range(NB):
                pool.wait_ge(s_rstd, J + 1)
                if J >= 4:
                    pool.wait_ge(s_out[J % 4], LOAD * (J // 4))
                nc.gpsimd.tensor_tensor(o[J % 4][:, :, :], y[J % 4][:, :, :], bc(rstd, J, D), ALU.mult) \
                    .then_inc(s_o, 1)

        @block.scalar
        def _(act):
            act.dma_start(wrow[:, :], w[:, :]).then_inc(s_w, 16)
            act.dma_start(bcol[:, :], b.rearrange("(o n) -> o n", o=1).to_broadcast([P, 1])).then_inc(s_b, 16)
            act.dma_start(biasb[:, :], bias.rearrange("(o n) -> o n", o=1).to_broadcast([P, D])).then_inc(s_bias, 16)
            act.wait_ge(s_b, 16)
            nc.scalar.activation(scale[:, :], bcol[:, :], ACT.Copy, scale=1.0 / (8.0 * SPLIT * SPLIT)) \
                .then_inc(s_scale, 1)
            act.wait_ge(s_x[0], 16 * 2 * C)
            act.wait_ge(s_x[1], 16 * 2 * C)
            nc.scalar.activation(squares[0][:, 0:2], x_pairs[:, :, 0], ACT.Square).then_inc(s_sq, 1)
            nc.scalar.activation(squares[0][:, 2:4], x_pairs[:, 0, 1:3], ACT.Square).then_inc(s_sq, 1)
            act.wait_ge(s_ssq, 1)
            nc.scalar.activation(pairs_of(root, 0, 1), pairs_of(ssq, 0, 1), ACT.Sqrt).then_inc(s_root, 1)
            nc.scalar.activation(squares[1][:, 0:1], x_pairs[:, 0, 3:4], ACT.Square).then_inc(s_sq, 1)
            nc.scalar.activation(squares[1][:, 1:4], x_pairs[:, 1, 1:4], ACT.Square).then_inc(s_sq, 1)
            act.wait_ge(s_ssq, 5)
            nc.scalar.activation(pairs_of(root, 1, FAR), pairs_of(ssq, 1, FAR), ACT.Sqrt).then_inc(s_root, 1)

            def operands(k):
                for h in range(2):
                    act.wait_ge(s_xT, 2 * k + h + 1)
                    nc.scalar.activation(xhi[:, block_of(k + FAR * h), :].rearrange("p c n -> p (c n)"),
                                         S[:, h, :], ACT.Copy).then_inc(s_hi, 1)
                    if k >= 1 and h == 0:
                        act.wait_ge(s_z, 2 * k)
                        act.wait_ge(s_loV, k)
                        act.wait_ge(s_loP, k)
                    nc.scalar.activation(xsT[h][:, :], S[:, h, :], ACT.Copy).then_inc(s_cpT, 1)

            operands(0)
            act.wait_ge(s_scale, 1)
            act.wait_ge(s_const, 3)

            def copy_v(dst, blk, s_done):
                act.dma_start(dst[:, :, :], v[:, bass.ds(blk * C, C), :]).then_inc(s_done, 16)

            def step(t, p1, p2):
                if p1 is not None and p1["new_I"]:
                    if not isinstance(p1["pairs"], int) or p1["pairs"] > 1:
                        act.wait_ge(s_xagg, p1["pairs"] - 1)
                    copy_v(vI, p1["I"], s_vI)
                k = place_of(t)
                if k is not None and k < FAR:
                    act.wait_ge(s_v, 2 * k + 2)
                if not t["early"]:
                    act.wait_ge(s_dagg, p2["g"] + 1)
                copy_v(vJ[t["slot"]], t["J"], s_vJ[t["slot"]])
                for h in range(2):
                    half = S[:, 2 * h:2 * h + 2, :]
                    act.wait_ge(s_S, t["g"] * 2 + (h + 1))
                    nc.scalar.activation(half, half, ACT.Tanh, scale=scale[:, :]).then_inc(s_tanh, 1)
                    if h == 0 and not t["early"]:
                        act.wait_ge(s_dmV, p2["g"] * 2 + 2)
                        act.wait_ge(s_dmP, p2["g"] * 2 + 2)
                        act.wait_ge(s_ET, p2["pairs"] * C)
                    act.wait_ge(s_tanh, t["g"] * 2 + (h + 1))
                    nc.scalar.activation(E[t["slot"]][:, 2 * h:2 * h + 2, :], half, ACT.Exp, scale=8.0) \
                        .then_inc(s_E, 1)
                if k is not None and k + 1 < FAR:
                    operands(k + 1)
                if k is not None and k >= FAR:
                    for J in (2 * (k - FAR), 2 * (k - FAR) + 1):
                        act.wait_ge(s_xb, J + 1)
                        if J >= 1:
                            act.wait_ge(s_xmean, J)
                        for m in range(C * J, C * J + C):
                            done = nc.scalar.activation(junk[:, m % C, :], xrow[:, m, :], ACT.Copy, scale=1.0 / D,
                                                        accum_out=xmean[:, m:m + 1])
                        done.then_inc(s_xmean, 1)

            run(act, step)
            act.wait_ge(s_xmean, NB)
            for J in range(NB):
                act.wait_ge(s_y, J + 1)
                for c in range(C):
                    m = C * J + c
                    done = nc.scalar.activation(junk[:, c, :], y[J % 4][:, c, :], ACT.Square,
                                                accum_out=var[:, m:m + 1])
                done.then_inc(s_ssy, 1)
                act.wait_ge(s_ssy, J + 1)
                nc.scalar.activation(std[:, block_of(J)], var[:, block_of(J)], ACT.Sqrt, scale=1.0 / D,
                                     bias=epsc[:, :]).then_inc(s_std, 1)

        @block.vector
        def _(dve):
            def summed(where, what):
                nc.vector.tensor_reduce(where, what, axis=AX.X, op=ALU.add).then_inc(s_ssq, 1)

            def norms(first, last):
                part = lambda t: pairs_of(t, first, last)
                n = 5 if first else 0
                dve.wait_ge(s_root, 2 if first else 1)
                nc.vector.reciprocal(part(quo), part(root)).then_inc(s_nrm, 1)
                dve.wait_ge(s_nrm, n + 1)
                nc.vector.tensor_tensor(part(quo), part(quo), part(ssq), ALU.mult).then_inc(s_nrm, 1)
                dve.wait_ge(s_nrm, n + 2)
                nc.vector.tensor_tensor(part(quo), part(quo), part(root), ALU.add).then_inc(s_nrm, 1)
                dve.wait_ge(s_nrm, n + 3)
                nc.vector.tensor_scalar(part(vn), part(quo), 0.5 / SPLIT, None, ALU.mult).then_inc(s_nrm, 1)
                dve.wait_ge(s_nrm, n + 4)
                nc.vector.reciprocal(part(rn), part(vn)).then_inc(s_nrm, 1)
                dve.wait_ge(s_nrm, n + 5)

            def scaled(k):
                for J in (k, k + FAR):
                    nc.vector.tensor_tensor(xs[:, block_of(J), :], xrow[:, block_of(J), :], bc(rn, J, D), ALU.mult) \
                        .then_inc(s_xs, 1)

            def lower_part(k):
                dve.wait_ge(s_cpT, 2 * k + 1)
                nc.vector.tensor_tensor(xlo[:, block_of(k), :].rearrange("p c n -> p (c n)"), xsT[0][:, :],
                                        xhi[:, block_of(k), :].rearrange("p c n -> p (c n)"), ALU.subtract) \
                    .then_inc(s_loV, 1)

            def projected(k):
                for h in range(2):
                    J = k + FAR * h
                    dve.wait_ge(s_z, 2 * k + h + 1)
                    nc.vector.tensor_tensor(v[:, block_of(J), 0:F],
                                            S[:, 2 + h, :].rearrange("p (c n) -> p c n", n=D)[:, :, 0:F],
                                            bc(vn, J, F), ALU.mult).then_inc(s_v, 1)

            dve.wait_ge(s_sq, 1)
            summed(pairs_of(ssq, 0, 1)[:, :, 0], squares[0][:, 0:2])
            norms(0, 1)
            scaled(0)
            dve.wait_ge(s_sq, 2)
            summed(ssq[:, C:3 * C], squares[0][:, 2:4].rearrange("p j c n -> p (j c) n"))
            dve.wait_ge(s_sq, 3)
            summed(ssq[:, 3 * C:4 * C], squares[1][:, 0])
            dve.wait_ge(s_sq, 4)
            summed(ssq[:, 5 * C:7 * C], squares[1][:, 1:3].rearrange("p j c n -> p (j c) n"))
            summed(ssq[:, 7 * C:8 * C], squares[1][:, 3])
            dve.wait_ge(s_wT, 1)
            nc.vector.tensor_reduce(wsum[:, :], accD[:, 0:P], axis=AX.X, op=ALU.add).then_inc(s_wc, 1)
            dve.wait_ge(s_wc, 1)
            nc.vector.tensor_scalar(wmean[:, :], wsum[:, :], 1.0 / D, None, ALU.mult).then_inc(s_wc, 1)
            dve.wait_ge(s_wc, 2)
            nc.vector.tensor_scalar(wcT[:, :], accD[:, 0:P], wmean[:, 0:1], None, ALU.subtract).then_inc(s_wc, 1)
            lower_part(0)
            norms(1, FAR)
            scaled(1)
            projected(0)
            scaled(2)
            scaled(3)
            dve.wait_ge(s_const, 3)

            def transposes(place, dst):
                slot, arrived, _ = place
                dve.wait_ge(s_raw[slot], arrived)
                nc.vector.transpose(dst[:, :, :].rearrange("p c (k q r) -> p c q k r", q=P // Q, r=Q),
                                    raw[slot][:, :, :].rearrange("p i (c r) -> p c i r", r=Q)).then_inc(s_tr, 1)

            def add(total, rows, done):
                part = acc[:, bass.ds(rows * B, B)]
                nc.vector.tensor_tensor(part, total[:, :], part, ALU.add).then_inc(done, 1)

            def adds(p):
                if p["pair"]:
                    dve.wait_ge(s_xagg, p["pairs"])
                    if not isinstance(p["pairs"], int) or p["pairs"] > 1:
                        dve.wait_ge(s_addX, p["pairs"] - 1)
                        dve.wait_ge(s_addD, p["group"])
                    add(accX, p["J"], s_addX)
                if p["closes"]:
                    dve.wait_ge(s_dagg, p["g"] + 1)
                    dve.wait_ge(s_addX, p["pairs"])
                    if not isinstance(p["group"], int) or p["group"] > 0:
                        dve.wait_ge(s_addD, p["group"])
                    add(accD, p["I"], s_addD)

            def step(t, p1, p2):
                s = t["slot"]
                if not t["early"]:
                    dve.wait_ge(s_dagg, p2["g"] + 1)
                transposes(t["raw"][0], dT[s])
                if p2 is not None:
                    adds(p2)
                if t["pair"]:
                    if not t["early"]:
                        dve.wait_ge(s_xagg, p2["pairs"])
                    transposes(t["raw"][1], xT[s])
                dve.wait_ge(s_E, t["g"] * 2 + 1)
                dve.wait_ge(s_tr, t["raw"][-1][2] + 1)
                for c in range(C // 2):
                    nc.vector.tensor_tensor(dT[s][:, c, :], E[s][:, c, :], dT[s][:, c, :], ALU.mult) \
                        .then_inc(s_dmV, 1)
                if t["pair"]:
                    for c in range(C):
                        k = place_of(t)
                        if c == 2 and k is not None and k + 1 < FAR:
                            lower_part(k + 1)
                            projected(k + 1)
                        dve.wait_ge(s_ET, (t["pairs"] - 1) * C + (c + 1))
                        nc.vector.tensor_tensor(xT[s][:, c, :], ET[c % 2][:, :], xT[s][:, c, :], ALU.mult) \
                            .then_inc(s_xm, 1)

            run(dve, step)
            adds(last[-2])
            adds(last[-1])
            dve.wait_ge(s_xc, NB)
            for J in range(NB):
                sums = final_of(J)[:, :, :, D]
                dve.wait_ge(s_fT, J + 1)
                nc.vector.reciprocal(rs[:, block_of(J)].rearrange("p (a c) -> p a c", a=2), sums).then_inc(s_rs, 1)
                dve.wait_ge(s_rs, J + 1)
                if J >= 4:
                    dve.wait_ge(s_o, J - 3)
                for c in range(C):
                    m = C * J + c
                    done = nc.vector.scalar_tensor_tensor(y[J % 4][:, c, :], final_of(J)[:, c // 2, c % 2, 0:D],
                                                          rs[:, m:m + 1], xrow[:, m, :], ALU.mult, ALU.add)
                done.then_inc(s_y, 1)
                if J >= 1:
                    dve.wait_ge(s_std, J)
                    nc.vector.reciprocal(rstd[:, block_of(J - 1)], std[:, block_of(J - 1)]).then_inc(s_rstd, 1)
            dve.wait_ge(s_std, NB)
            nc.vector.reciprocal(rstd[:, block_of(NB - 1)], std[:, block_of(NB - 1)]).then_inc(s_rstd, 1)

        @block.tensor
        def _(pe):
            pe.wait_ge(s_id, 7)
            pe.wait_ge(s_w, 16)
            nc.tensor.transpose(accD[:, 0:P], wrow[:, :], ident[:, :]).then_inc(s_wT, 1)

            def transpose_x(k):
                if k >= 1:
                    pe.wait_ge(s_E, 2 * k)
                for h in range(2):
                    pe.wait_ge(s_xs, 2 * k + h + 1)
                    for c in range(C):
                        done = nc.tensor.transpose(S[:, h, P * c:P * c + P], xs[:, C * (k + FAR * h) + c, :],
                                                   ident[:, :])
                    done.then_inc(s_xT, 1)

            def project(k):
                if k == 0:
                    pe.wait_ge(s_wc, 3)
                for h in range(2):
                    pe.wait_ge(s_cpT, 2 * k + h + 1)
                    for c in range(C):
                        done = nc.tensor.matmul(S[:, 2 + h, P * c:P * c + P], xsT[h][:, P * c:P * c + P],
                                                wcT[:, :], start=True, stop=True)
                    done.then_inc(s_z, 1)

            transpose_x(0)
            project(0)

            def moving(part, blk):
                return part[:, bass.ds(blk * C, C), :].rearrange("p c n -> p (c n)")

            def cosines(t):
                k = place_of(t)
                if k is not None and k < FAR:
                    pe.wait_ge(s_cpT, 2 * k + 2)
                    pe.wait_ge(s_loV, k + 1)
                    pe.wait_ge(s_loP, k + 1)
                for c in range(C):
                    if k is not None and k < FAR and c == 2:
                        pe.wait_ge(s_v, 2 * k + 2)
                    if not (isinstance(t["g"], int) and t["g"] == 0) and c % 2 == 0:
                        pe.wait_ge(s_E, t["g"] * 2 - 1 + c // 2)
                    for n, (left, right) in enumerate(((xhi, xhi), (xhi, xlo), (xlo, xhi))):
                        done = nc.tensor.matmul(S[:, c, :], left[:, t["J"] * C + c, :], moving(right, t["I"]),
                                                start=n == 0, stop=n == 2)
                    if c % 2:
                        done.then_inc(s_S, 1)

            def aggregate_d(p):
                pe.wait_ge(s_vJ[p["slot"]], (p["turn"] + 1) * 16)
                if p["opens"] and not (isinstance(p["group"], int) and p["group"] == 0):
                    pe.wait_ge(s_addD, p["group"])
                for c in range(C):
                    if c == 0:
                        pe.wait_ge(s_dmV, p["g"] * 2 + 2)
                    if c == C // 2:
                        pe.wait_ge(s_dmP, p["g"] * 2 + 2)
                    done = nc.tensor.matmul(accD[:, :], vJ[p["slot"]][:, c, :], dT[p["slot"]][:, c, :],
                                            start=p["opens"] and c == 0, stop=p["closes"] and c == C - 1)
                done.then_inc(s_dagg, 1)

            def aggregate_x(p, h):
                if h == 0:
                    pe.wait_ge(s_vI, p["vI"] * 16)
                    if not isinstance(p["pairs"], int) or p["pairs"] > 1:
                        pe.wait_ge(s_addX, p["pairs"] - 1)
                    pe.wait_ge(s_xm, p["pairs"] * C)
                for c in range(2 * h, 2 * h + 2):
                    done = nc.tensor.matmul(accX[:, :], vI[:, c, :], xT[p["slot"]][:, c, :],
                                            start=c == 0, stop=c == C - 1)
                if h == 1:
                    done.then_inc(s_xagg, 1)

            def transpose_E(t, h):
                pe.wait_ge(s_E, t["g"] * 2 + 2)
                for k in range(2 * h, 2 * h + 2):
                    if k < 2:
                        if isinstance(t["pairs"], int) and t["pairs"] == 1:
                            pass
                        else:
                            pe.wait_ge(s_xm, (t["pairs"] - 1) * C - (1 - k))
                    else:
                        pe.wait_ge(s_xm, (t["pairs"] - 1) * C + (k - 1))
                    for c in range(C):
                        done = nc.tensor.transpose(ET[k % 2][:, P * c:P * c + P],
                                                   E[t["slot"]][:, c, P * k:P * k + P], ident[:, :])
                    done.then_inc(s_ET, 1)

            def step(t, p1, p2):
                cosines(t)
                if p1 is not None:
                    aggregate_d(p1)
                k = place_of(t)
                more = k is not None and k + 1 < FAR
                for h in range(2):
                    if more and h == 1:
                        project(k + 1)
                    if t["pair"]:
                        transpose_E(t, h)
                    if more and h == 0:
                        transpose_x(k + 1)
                    if p1 is not None and p1["pair"]:
                        aggregate_x(p1, h)

            run(pe, step)
            aggregate_d(last[-1])
            aggregate_x(last[-1], 0)
            aggregate_x(last[-1], 1)
            pe.wait_ge(s_addX, last[-1]["pairs"])
            pe.wait_ge(s_addD, last[-1]["group"] + 1)
            for J in range(NB):
                if J >= 2:
                    pe.wait_ge(s_y, J - 1)
                for c in range(C):
                    m = C * J + c
                    done = nc.tensor.matmul(final_of(J)[:, c // 2, c % 2, 0:D + 1], acc[:, P * m:P * m + P],
                                            restore[:, :], start=True, stop=True)
                done.then_inc(s_fT, 1)


def kernel(x, adj, L0_gnn_W, L0_gnn_bias, L0_gnn_b):
    import numpy as np
    import concourse.bacc as bacc
    from concourse.bass_utils import run_bass_kernel_spmd

    nc = bacc.Bacc("TRN2", target_bir_lowering=False, num_devices=1)
    arrays = dict(x=x, adj=adj, w=L0_gnn_W, bias=L0_gnn_bias, b=L0_gnn_b)
    arrays = {f"in_{k}": np.ascontiguousarray(a) for k, a in arrays.items()}
    ins = [nc.dram_tensor(k, a.shape, mybir.dt.from_np(a.dtype), kind="ExternalInput").ap() for k, a in arrays.items()]
    out = nc.dram_tensor("out", x.shape, mybir.dt.float32, kind="ExternalOutput").ap()
    adj_attention_layernorm(nc, *ins, out)
    return run_bass_kernel_spmd(nc, [arrays], core_ids=[0]).results[0]["out"]
```

```python
import concourse.bass as bass
from concourse import mybir
from contextlib import ExitStack



def adj_attention_layernorm(nc, x, adj, w, bias, b, out):
    fp32 = mybir.dt.float32
    fp16 = mybir.dt.float16
    ALU = mybir.AluOpType
    ACT = mybir.ActivationFunctionType
    AX = mybir.AxisListType

    N, D = x.shape
    P = 128
    Q = 32
    B = 512
    NB = N // B
    C = B // P
    NC = N // P
    F = D - 1
    SPLIT = 2.0 ** 12
    EPS = 1e-5
    WARM = 21
    NEAR = 3
    UNITS = 1 + NEAR
    FAR = NB // 2
    ABLK = 1 + 2 * NEAR
    RING = ABLK
    LOAD = 16 * (P // Q)

    ctx = ExitStack()
    with ctx:
        def sb(name, shape, dt=fp32):
            return ctx.enter_context(nc.sbuf_tensor(name, shape, dt))

        def pb(name, shape, dt=fp32):
            return ctx.enter_context(nc.psum_tensor(name, shape, dt))

        def sem(name):
            return ctx.enter_context(nc.semaphore(name))

        xrow = sb("xrow", [P, NC, D])
        xs = sb("xs", [P, NC, D])
        xhi = sb("xhi", [P, NC, P], fp16)
        xlo = sb("xlo", [P, NC, P], fp16)
        v = sb("v", [P, NC, D])
        acc = sb("acc", [P, N])
        raw = [sb(f"raw{s}", [P, B // Q, P]) for s in range(RING)]
        dT = [sb(f"dT{s}", [P, C, B]) for s in range(2)]
        xT = [sb(f"xT{s}", [P, C, B]) for s in range(2)]
        E = [sb(f"E{s}", [P, C, B]) for s in range(2)]
        vJ = [sb(f"vJ{s}", [P, C, D]) for s in range(2)]
        vI = sb("vI", [P, C, D])
        xsT = [sb(f"xsT{s}", [P, B]) for s in range(2)]
        ident = sb("ident", [P, P])
        restore = sb("restore", [P, D + 1])
        wrow = sb("wrow", [P, P])
        wcT = sb("wcT", [P, P])
        wsum = sb("wsum", [P, 1])
        wmean = sb("wmean", [P, 1])
        bcol = sb("bcol", [P, 1])
        scale = sb("scale", [P, 1])
        biasb = sb("biasb", [P, D])
        ssq = sb("ssq", [P, NC])
        root = sb("root", [P, NC])
        nrm = sb("nrm", [P, NC])
        quo = sb("quo", [P, NC])
        rn = sb("rn", [P, NC])
        vn = sb("vn", [P, NC])
        rs = sb("rs", [P, NC])
        var = sb("var", [P, NC])
        std = sb("std", [P, NC])
        rstd = sb("rstd", [P, NC])
        xmean = sb("xmean", [P, NC])
        epsc = sb("epsc", [P, 1])
        warm = sb("warm", [P, 4])
        y = xs
        junk = sb("junk", [P, C, D])

        S = pb("S", [P, C, B])
        ET = [pb(f"ET{s}", [P, B]) for s in range(2)]
        accD = pb("accD", [P, B])
        accX = pb("accX", [P, B])

        s_x = [sem(f"s_x{J}") for J in range(NB)]
        s_raw = [sem(f"s_raw{s}") for s in range(RING)]
        s_vJ = [sem(f"s_vJ{s}") for s in range(2)]
        s_out = sem("s_out")
        s_w = sem("s_w")
        s_b = sem("s_b")
        s_bias = sem("s_bias")
        s_const = sem("s_const")
        s_id = sem("s_id")
        s_sq = sem("s_sq")
        s_ssq = sem("s_ssq")
        s_root = sem("s_root")
        s_eps = sem("s_eps")
        s_warm = sem("s_warm")
        s_nrm = sem("s_nrm")
        s_xs = sem("s_xs")
        s_wT = sem("s_wT")
        s_wc = sem("s_wc")
        s_xT = sem("s_xT")
        s_hi = sem("s_hi")
        s_cpT = sem("s_cpT")
        s_loV = sem("s_loV")
        s_loP = sem("s_loP")
        s_z = sem("s_z")
        s_v = sem("s_v")
        s_S = sem("s_S")
        s_tanh = sem("s_tanh")
        s_E = sem("s_E")
        s_tr = sem("s_tr")
        s_ET = sem("s_ET")
        s_dmV = sem("s_dmV")
        s_dmP = sem("s_dmP")
        s_xm = sem("s_xm")
        s_dagg = sem("s_dagg")
        s_xagg = sem("s_xagg")
        s_addD = sem("s_addD")
        s_addX = sem("s_addX")
        s_add_end = sem("s_add_end")
        s_vI = sem("s_vI")
        s_scale = sem("s_scale")
        s_xb = sem("s_xb")
        s_xmean = sem("s_xmean")
        s_xc = sem("s_xc")
        s_fT = sem("s_fT")
        s_rs = sem("s_rs")
        s_y = sem("s_y")
        s_ssy = sem("s_ssy")
        s_std = sem("s_std")
        s_rstd = sem("s_rstd")
        s_o = sem("s_o")
        s_o_end = sem("s_o_end")

        block = ctx.enter_context(nc.Block())

        def block_of(J):
            return slice(C * J, C * J + C)

        def bc(t, J, n):
            return t[:, block_of(J)].unsqueeze(2).to_broadcast([P, C, n])

        def pair(t, k):
            return t[:, :].rearrange("p (h j c) -> p h j c", h=2, c=C)[:, :, k]

        ring_uses = [0] * RING
        far_raw = []
        for k in range(2 * FAR):
            ring_uses[(k - 1) % RING] += 1
            far_raw.append(((k - 1) % RING, LOAD * ring_uses[(k - 1) % RING], k))

        def far_unit(k):
            return dict(g=k, I=k, J=k + FAR, pair=True, pairs=k + 1, group=k, opens=True, closes=True, slot=k % 2,
                        raw=far_raw[2 * k:2 * k + 2], early=k < 2)

        def near_unit(I, u, J=None):
            first = 2 * u - 1 if u else 0
            if J is None:
                J = (I + u) & (NB - 1) if u else I
            return dict(g=FAR + UNITS * I + u, I=I, J=J, pair=u > 0,
                        pairs=FAR + NEAR * I + u, group=FAR + I, opens=u == 0, closes=u == NEAR, slot=u % 2,
                        turn=UNITS // 2 * (I - 1) + u // 2 + u % 2,
                        raw=[(s, (I + ring_uses[s] + 1) * LOAD, 2 * FAR + ABLK * I + s)
                             for s in range(first, first + (2 if u else 1))],
                        new_I=u == 1, vI=I + 1, early=False)

        straight = [far_unit(k) for k in range(FAR)] + [near_unit(0, u) for u in range(UNITS)]
        last = [near_unit(NB - 1, u) for u in range(UNITS)]

        def place_of(t):
            return t["g"] if isinstance(t["g"], int) and t["g"] < FAR + UNITS else None

        def last_place_of(t):
            return t["g"] - last[0]["g"] if isinstance(t["g"], int) and t["g"] >= last[0]["g"] else None

        FINAL = [NEAR + u for u in range(UNITS)] + [0, 1, NB - 1, 2]
        EARLY = UNITS
        TOGETHER = EARLY - 1
        together = slice(C * FINAL[0], C * FINAL[TOGETHER - 1] + C)

        def roots_up_to(n):
            return max(n - TOGETHER + 1, 0) + 1

        def final_of(n):
            half = 1 if n < EARLY else n % 2
            return S[:, 2 * half:2 * half + 2, 0:2 * (D + 2)].rearrange("p a (c n) -> p a c n", c=2)

        x_pairs = xrow[:, :, :].rearrange("p (h j c) d -> p h j c d", h=2, c=C)

        def transposed_of(k, h):
            return (accD, accX)[h][:, :] if k == 1 else S[:, h, :]

        def projection_of(k, h):
            return ET[h][:, :] if k == 0 else (accD, accX)[h][:, :] if k == 1 else S[:, 2 + h, :]

        squares_pairs = xs[:, :, :].rearrange("p (h j c) d -> p h j c d", h=2, c=C)

        def run(engine, step):
            for k, t in enumerate(straight):
                step(t, straight[k - 1] if k >= 1 else None, straight[k - 2] if k >= 2 else None)
            J_regs = [engine.alloc_register(f"J{u}") for u in range(1, UNITS)]
            with engine.Fori(1, NB - 1) as I:
                p2, p1 = near_unit(I - 1, UNITS - 2), near_unit(I - 1, UNITS - 1)
                for u in range(UNITS):
                    J = I
                    if u:
                        engine.reg_alu(J_regs[u - 1], I, u, ALU.add)
                        engine.reg_alu(J_regs[u - 1], J_regs[u - 1], NB - 1, ALU.bitwise_and)
                        J = engine.snap(J_regs[u - 1], min_val=0, max_val=NB - 1)
                    t = near_unit(I, u, J)
                    step(t, p1, p2)
                    p2, p1 = p1, t
            line = [near_unit(NB - 2, UNITS - 2), near_unit(NB - 2, UNITS - 1)] + last
            for k in range(2, len(line)):
                step(line[k], line[k - 1], line[k - 2])

        @block.sync
        def _(sp):
            def load_x(k):
                for J in (k, k + FAR):
                    for q in range(P // Q):
                        src = x[J * B + P * q:J * B + P * q + P, :].rearrange("(c r) d -> r c d", r=Q)
                        sp.dma_start(xrow[Q * q:Q * q + Q, block_of(J), :], src).then_inc(s_x[J], 16)

            sp.dma_start(wrow[:, :], w[:, :]).then_inc(s_w, 16)
            load_x(0)
            load_x(1)
            sp.dma_start(bcol[:, :], b.rearrange("(o n) -> o n", o=1).to_broadcast([P, 1])).then_inc(s_b, 16)

            def load(place, rows, cols):
                slot, _, before = place
                if not isinstance(before, int) or before >= RING:
                    sp.wait_ge(s_tr, before - RING + 1)
                for q in range(P // Q):
                    src = adj[bass.ds(rows * B, B), bass.ds(cols * B + P * q, P)]
                    sp.dma_start(raw[slot][Q * q:Q * q + Q, :, :], src.rearrange("(i r) n -> r i n", r=Q)) \
                        .then_inc(s_raw[slot], 16)

            def step(t, p1, p2):
                load(t["raw"][0], t["I"], t["J"])
                if t["pair"]:
                    load(t["raw"][1], t["J"], t["I"])
                if place_of(t) == 0:
                    sp.dma_start(biasb[:, :], bias.rearrange("(o n) -> o n", o=1).to_broadcast([P, D])) \
                        .then_inc(s_bias, 16)
                    for k in range(2, FAR):
                        load_x(k)

            run(sp, step)
            for n, J in enumerate(FINAL):
                if n < NB - 2:
                    sp.wait_ge(s_o, n + 1)
                else:
                    sp.wait_ge(s_o_end, n - (NB - 2) + 1)
                for q in range(P // Q):
                    dst = out[J * B + P * q:J * B + P * q + P, :].rearrange("(c r) d -> r c d", r=Q)
                    sp.dma_start(dst, y[Q * q:Q * q + Q, block_of(J), :]).then_inc(s_out, 16)
            sp.wait_ge(s_out, LOAD * NB)

        @block.gpsimd
        def _(pool):
            nc.gpsimd.memset(ident[:, :], 0.0).then_inc(s_id, 1)
            nc.gpsimd.memset(restore[:, :], 0.0).then_inc(s_id, 1)
            pool.wait_ge(s_id, 2)
            nc.gpsimd.affine_select(out=ident[:, :], in_=ident[:, :], compare_op=ALU.not_equal, fill=1.0, base=0,
                                    pattern=[[-1, P]], channel_multiplier=1).then_inc(s_id, 1)
            nc.gpsimd.affine_select(out=restore[:, 0:F], in_=restore[:, 0:F], compare_op=ALU.not_equal, fill=1.0,
                                    base=0, pattern=[[-1, F]], channel_multiplier=1).then_inc(s_id, 1)
            nc.gpsimd.memset(restore[:, F:D], -1.0).then_inc(s_id, 1)
            pool.wait_ge(s_id, 5)
            nc.gpsimd.affine_select(out=restore[:, F:D], in_=restore[:, F:D], compare_op=ALU.not_equal, fill=0.0,
                                    base=-F, pattern=[[0, 1]], channel_multiplier=1).then_inc(s_id, 1)
            nc.gpsimd.affine_select(out=restore[:, D:D + 1], in_=restore[:, D:D + 1], compare_op=ALU.not_equal,
                                    fill=1.0, base=-F, pattern=[[0, 1]], channel_multiplier=1).then_inc(s_id, 1)
            nc.gpsimd.memset(v[:, :, F:D], 1.0).then_inc(s_const, 1)
            nc.gpsimd.memset(acc[:, :], 0.0).then_inc(s_const, 1)

            def lower_part(k):
                pool.wait_ge(s_cpT, 2 * k + 2)
                rows = block_of(k + FAR)
                nc.gpsimd.tensor_tensor(xlo[:, rows, :].rearrange("p c n -> p (c n)"), xsT[1][:, :],
                                        xhi[:, rows, :].rearrange("p c n -> p (c n)"), ALU.subtract) \
                    .then_inc(s_loP, 1)

            def scaled(k):
                pool.wait_ge(s_nrm, 5 * k + 5)
                for J in (k, k + FAR):
                    nc.gpsimd.tensor_tensor(xs[:, block_of(J), :], xrow[:, block_of(J), :], bc(rn, J, D), ALU.mult) \
                        .then_inc(s_xs, 1)

            scaled(1)

            def step(t, p1, p2):
                if place_of(t) in range(1, FAR - 1):
                    scaled(place_of(t) + 1)
                pool.wait_ge(s_tr, t["raw"][0][2] + 1)
                pool.wait_ge(s_E, t["g"] * 2 + 2)
                for c in range(C // 2, C):
                    nc.gpsimd.tensor_tensor(dT[t["slot"]][:, c, :], E[t["slot"]][:, c, :], dT[t["slot"]][:, c, :],
                                            ALU.mult).then_inc(s_dmP, 1)
                k = place_of(t)
                if k is not None and k < FAR:
                    if k + 1 < FAR:
                        lower_part(k + 1)
                    pool.wait_ge(s_xs, 2 * k + 2)
                    if k == 0:
                        pool.wait_ge(s_bias, 16)
                    for J in (k, k + FAR):
                        part = xrow[:, block_of(J), :]
                        nc.gpsimd.tensor_tensor(part, part, biasb[:, :].unsqueeze(1).to_broadcast([P, C, D]),
                                                ALU.add).then_inc(s_xb, 1)
                elif k is not None:
                    for n, J in enumerate((k - FAR, k)):
                        pool.wait_ge(s_xmean, 2 * (k - FAR) + n + 1)
                        part = xrow[:, block_of(J), :]
                        nc.gpsimd.tensor_tensor(part, part, bc(xmean, J, D), ALU.subtract).then_inc(s_xc, 1)

            run(pool, step)
            for n, J in enumerate(FINAL[:-2]):
                pool.wait_ge(s_rstd, roots_up_to(n))
                nc.gpsimd.tensor_tensor(y[:, block_of(J), :], y[:, block_of(J), :], bc(rstd, J, D), ALU.mult) \
                    .then_inc(s_o, 1)

        @block.scalar
        def _(act):
            act.wait_ge(s_eps, 1)

            def table_of(func, n):
                nc.scalar.activation(warm[:, n:n + 1], epsc[:, :], func).then_inc(s_warm, 1)

            table_of(ACT.Sqrt, 0)

            def squared(k):
                for J in (k, k + FAR):
                    act.wait_ge(s_x[J], LOAD)
                nc.scalar.activation(squares_pairs[:, :, k], x_pairs[:, :, k], ACT.Square).then_inc(s_sq, 1)

            def rooted(k):
                act.wait_ge(s_ssq, 2 * k + 2 if k < 2 else k + 3)
                nc.scalar.activation(pair(root, k), pair(ssq, k), ACT.Sqrt).then_inc(s_root, 1)

            def squared_and_summed(k, h):
                J = k + FAR * h
                act.wait_ge(s_x[J], LOAD)
                for c in range(C):
                    m = C * J + c
                    done = nc.scalar.activation(xs[:, m, :], xrow[:, m, :], ACT.Square,
                                                accum_out=ssq[:, m:m + 1])
                done.then_inc(s_ssq, 1)

            squared_and_summed(0, 0)
            squared_and_summed(0, 1)
            rooted(0)
            squared_and_summed(1, 0)

            def operands(k):
                for h in range(2):
                    act.wait_ge(s_xT, 2 * k + h + 1)
                    nc.scalar.activation(xhi[:, block_of(k + FAR * h), :].rearrange("p c n -> p (c n)"),
                                         transposed_of(k, h), ACT.Copy).then_inc(s_hi, 1)
                    if k >= 1 and h == 0:
                        act.wait_ge(s_z, 2 * k)
                        act.wait_ge(s_loV, k + 1)
                        if k >= 2:
                            act.wait_ge(s_loP, k - 1)
                    nc.scalar.activation(xsT[h][:, :], transposed_of(k, h), ACT.Copy).then_inc(s_cpT, 1)

            operands(0)
            squared_and_summed(1, 1)
            rooted(1)
            act.wait_ge(s_b, 16)
            nc.scalar.activation(scale[:, :], bcol[:, :], ACT.Copy, scale=1.0 / (8.0 * SPLIT * SPLIT)) \
                .then_inc(s_scale, 1)
            table_of(ACT.Tanh, 1)
            act.wait_ge(s_scale, 1)

            def copy_v(dst, blk, s_done):
                act.dma_start(dst[:, :, :], v[:, bass.ds(blk * C, C), :]).then_inc(s_done, 16)

            def step(t, p1, p2):
                k = place_of(t)
                in_loop = not isinstance(t["g"], int)
                if k == FAR + NEAR - 1:
                    act.wait_ge(s_v, NB)
                    act.wait_ge(s_const, 1)
                    copy_v(vI, 0, s_vI)
                if in_loop and p1["new_I"]:
                    act.wait_ge(s_xagg, p1["pairs"] - 1)
                    copy_v(vI, p1["I"], s_vI)
                if in_loop or k == FAR + NEAR:
                    act.wait_ge(s_dagg, p2["g"] + 1)
                    copy_v(vJ[t["slot"]], t["J"], s_vJ[t["slot"]])
                for h in range(2):
                    half = S[:, 2 * h:2 * h + 2, :]
                    act.wait_ge(s_S, t["g"] * 2 + (h + 1))
                    nc.scalar.activation(half, half, ACT.Tanh, scale=scale[:, :]).then_inc(s_tanh, 1)
                    if h == 0 and not t["early"]:
                        act.wait_ge(s_dmV, p2["g"] * 2 + 2)
                        act.wait_ge(s_dmP, p2["g"] * 2 + 2)
                        act.wait_ge(s_ET, p2["pairs"] * C)
                    act.wait_ge(s_tanh, t["g"] * 2 + (h + 1))
                    nc.scalar.activation(E[t["slot"]][:, 2 * h:2 * h + 2, :], half, ACT.Exp, scale=8.0) \
                        .then_inc(s_E, 1)
                if k is not None and k + 1 < FAR:
                    operands(k + 1)
                if k is not None and k + 2 < FAR:
                    squared(k + 2)
                    rooted(k + 2)
                    table_of(ACT.Tanh, k + 2)
                if k is not None and k >= FAR:
                    for n, J in enumerate((k - FAR, k)):
                        before = 2 * (k - FAR) + n
                        act.wait_ge(s_xb, before + 1)
                        if before >= 1:
                            act.wait_ge(s_xmean, before)
                        for m in range(C * J, C * J + C):
                            done = nc.scalar.activation(junk[:, m % C, :], xrow[:, m, :], ACT.Copy, scale=1.0 / D,
                                                        accum_out=xmean[:, m:m + 1])
                        done.then_inc(s_xmean, 1)
                n = last_place_of(t)
                if n == TOGETHER:
                    deviation(n - 1, together)
                if n is not None:
                    variance(n)

            def variance(n):
                if n == 0:
                    act.wait_ge(s_xmean, NB)
                else:
                    act.wait_ge(s_ssy, n)
                for c in range(C):
                    m = C * FINAL[n] + c
                    act.wait_ge(s_y, C * n + c + 1)
                    done = nc.scalar.activation(junk[:, m % C, :], y[:, m, :], ACT.Square, accum_out=var[:, m:m + 1])
                done.then_inc(s_ssy, 1)

            def deviation(n, chunks):
                act.wait_ge(s_ssy, n + 1)
                nc.scalar.activation(std[:, chunks], var[:, chunks], ACT.Sqrt, scale=1.0 / D, bias=epsc[:, :]) \
                    .then_inc(s_std, 1)

            run(act, step)
            for n in range(TOGETHER, NB):
                if n > TOGETHER:
                    variance(n)
                deviation(n, block_of(FINAL[n]))

        @block.vector
        def _(dve):
            def summed(k):
                dve.wait_ge(s_sq, k - 1)
                nc.vector.tensor_reduce(pair(ssq, k), squares_pairs[:, :, k], axis=AX.X, op=ALU.add).then_inc(s_ssq, 1)

            def norms(k):
                n = 5 * k
                dve.wait_ge(s_root, k + 1)
                nc.vector.reciprocal(pair(quo, k), pair(root, k)).then_inc(s_nrm, 1)
                dve.wait_ge(s_nrm, n + 1)
                nc.vector.tensor_tensor(pair(quo, k), pair(quo, k), pair(ssq, k), ALU.mult).then_inc(s_nrm, 1)
                dve.wait_ge(s_nrm, n + 2)
                nc.vector.tensor_tensor(pair(quo, k), pair(quo, k), pair(root, k), ALU.add).then_inc(s_nrm, 1)
                dve.wait_ge(s_nrm, n + 3)
                nc.vector.tensor_scalar(pair(vn, k), pair(quo, k), 0.5 / SPLIT, None, ALU.mult).then_inc(s_nrm, 1)
                dve.wait_ge(s_nrm, n + 4)
                nc.vector.reciprocal(pair(rn, k), pair(vn, k)).then_inc(s_nrm, 1)

            def lower_part(k, h=0):
                dve.wait_ge(s_cpT, 2 * k + h + 1)
                rows = block_of(k + FAR * h)
                nc.vector.tensor_tensor(xlo[:, rows, :].rearrange("p c n -> p (c n)"), xsT[h][:, :],
                                        xhi[:, rows, :].rearrange("p c n -> p (c n)"), ALU.subtract) \
                    .then_inc(s_loV, 1)

            def projected(k):
                for h in range(2):
                    J = k + FAR * h
                    dve.wait_ge(s_z, 2 * k + h + 1)
                    nc.vector.tensor_tensor(v[:, block_of(J), 0:F],
                                            projection_of(k, h).rearrange("p (c n) -> p c n", n=D)[:, :, 0:F],
                                            bc(vn, J, F), ALU.mult).then_inc(s_v, 1)

            nc.vector.memset(epsc[:, :], EPS).then_inc(s_eps, 1)
            dve.wait_ge(s_wT, 1)
            nc.vector.tensor_reduce(wsum[:, :], accD[:, 0:P], axis=AX.X, op=ALU.add).then_inc(s_wc, 1)
            dve.wait_ge(s_wc, 1)
            nc.vector.tensor_scalar(wmean[:, :], wsum[:, :], 1.0 / D, None, ALU.mult).then_inc(s_wc, 1)
            dve.wait_ge(s_wc, 2)
            nc.vector.tensor_scalar(wcT[:, :], accD[:, 0:P], wmean[:, 0:1], None, ALU.subtract).then_inc(s_wc, 1)
            norms(0)
            dve.wait_ge(s_nrm, 5)
            for J in (0, FAR):
                nc.vector.tensor_tensor(xs[:, block_of(J), :], xrow[:, block_of(J), :], bc(rn, J, D), ALU.mult) \
                    .then_inc(s_xs, 1)
            lower_part(0)
            lower_part(0, 1)
            norms(1)
            projected(0)
            dve.wait_ge(s_const, 2)

            def transposes(place, dst):
                slot, arrived, _ = place
                dve.wait_ge(s_raw[slot], arrived)
                nc.vector.transpose(dst[:, :, :].rearrange("p c (k q r) -> p c q k r", q=P // Q, r=Q),
                                    raw[slot][:, :, :].rearrange("p i (c r) -> p c i r", r=Q)).then_inc(s_tr, 1)

            def add(total, rows, done):
                part = acc[:, bass.ds(rows * B, B)]
                nc.vector.tensor_tensor(part, total[:, :], part, ALU.add).then_inc(done, 1)

            def add_d(p):
                dve.wait_ge(s_dagg, p["g"] + 1)
                dve.wait_ge(s_addX, p["pairs"] - 1)
                if not isinstance(p["group"], int) or p["group"] > 0:
                    dve.wait_ge(s_addD, p["group"])
                add(accD, p["I"], s_addD)

            def add_x(p):
                dve.wait_ge(s_xagg, p["pairs"])
                if not isinstance(p["pairs"], int) or p["pairs"] > 1:
                    dve.wait_ge(s_addX, p["pairs"] - 1)
                    dve.wait_ge(s_addD, p["group"])
                add(accX, p["J"], s_addX)

            def adds(p):
                if p["closes"]:
                    add_d(p)
                if p["pair"]:
                    add_x(p)

            def residual(n):
                J = FINAL[n]
                sums = final_of(n)[:, :, :, D]
                if n == 0:
                    dve.wait_ge(s_xc, NB)
                dve.wait_ge(s_fT, n + 1)
                nc.vector.reciprocal(rs[:, block_of(J)].rearrange("p (a c) -> p a c", a=2), sums).then_inc(s_rs, 1)
                dve.wait_ge(s_rs, n + 1)
                for c in range(C):
                    m = C * J + c
                    nc.vector.scalar_tensor_tensor(y[:, m, :], final_of(n)[:, c // 2, c % 2, 0:D], rs[:, m:m + 1],
                                                   xrow[:, m, :], ALU.mult, ALU.add).then_inc(s_y, 1)

            def reciprocal_of_std(n, chunks=None):
                chunks = chunks or block_of(FINAL[n])
                dve.wait_ge(s_std, roots_up_to(n))
                nc.vector.reciprocal(rstd[:, chunks], std[:, chunks]).then_inc(s_rstd, 1)

            def step(t, p1, p2):
                s = t["slot"]
                if place_of(t) in range(1, FAR - 1):
                    norms(place_of(t) + 1)
                if not t["early"]:
                    dve.wait_ge(s_dagg, p2["g"] + 1)
                far = place_of(t) in range(FAR)
                if p2 is not None and far:
                    adds(p2)
                transposes(t["raw"][0], dT[s])
                if p2 is not None and not far:
                    adds(p2)
                if t["pair"]:
                    if not t["early"]:
                        dve.wait_ge(s_xagg, p2["pairs"])
                    transposes(t["raw"][1], xT[s])
                dve.wait_ge(s_E, t["g"] * 2 + 1)
                dve.wait_ge(s_tr, t["raw"][-1][2] + 1)
                for c in range(C // 2):
                    nc.vector.tensor_tensor(dT[s][:, c, :], E[s][:, c, :], dT[s][:, c, :], ALU.mult) \
                        .then_inc(s_dmV, 1)
                k = place_of(t)
                n = last_place_of(t)
                if n == 0:
                    residual(n)
                if t["pair"]:
                    for c in range(C):
                        if c == 2 and k is not None and k + 1 < FAR:
                            lower_part(k + 1)
                        if c == 2 and k is not None and k + 2 < FAR:
                            summed(k + 2)
                        if c == 2 and k is not None and k + 1 < FAR:
                            projected(k + 1)
                        if c == 2 and n == TOGETHER:
                            reciprocal_of_std(n - 1, together)
                        if c == 2 and n is not None:
                            residual(n)
                        dve.wait_ge(s_ET, (t["pairs"] - 1) * C + (c + 1))
                        nc.vector.tensor_tensor(xT[s][:, c, :], ET[c % 2][:, :], xT[s][:, c, :], ALU.mult) \
                            .then_inc(s_xm, 1)

            run(dve, step)
            reciprocal_of_std(EARLY - 1)
            adds(last[-2])
            residual(EARLY)
            residual(EARLY + 1)
            reciprocal_of_std(EARLY)
            add_d(last[-1])
            reciprocal_of_std(EARLY + 1)
            dve.wait_ge(s_xagg, last[-1]["pairs"])
            dve.wait_ge(s_addX, last[-1]["pairs"] - 1)
            for c in range(C):
                part = acc[:, B * FINAL[-1] + P * c:B * FINAL[-1] + P * c + P]
                nc.vector.tensor_tensor(part, accX[:, P * c:P * c + P], part, ALU.add).then_inc(s_add_end, 1)
            residual(EARLY + 2)
            residual(EARLY + 3)
            for n in (NB - 2, NB - 1):
                reciprocal_of_std(n)
                dve.wait_ge(s_rstd, roots_up_to(n))
                rows = block_of(FINAL[n])
                nc.vector.tensor_tensor(y[:, rows, :], y[:, rows, :], bc(rstd, FINAL[n], D), ALU.mult) \
                    .then_inc(s_o_end, 1)

        @block.tensor
        def _(pe):
            pe.wait_ge(s_id, 7)
            pe.wait_ge(s_w, 16)
            nc.tensor.transpose(accD[:, 0:P], wrow[:, :], ident[:, :]).then_inc(s_wT, 1)
            for n in range(WARM):
                nc.tensor.matmul(accX[:, 0:P], ident[:, :], ident[:, :], start=n == 0, stop=n == WARM - 1)

            def transpose_x(k):
                if k >= 2:
                    pe.wait_ge(s_E, 2 * k)
                for h in range(2):
                    pe.wait_ge(s_xs, 2 * k + h + 1)
                    for c in range(C):
                        done = nc.tensor.transpose(transposed_of(k, h)[:, P * c:P * c + P],
                                                   xs[:, C * (k + FAR * h) + c, :], ident[:, :])
                    done.then_inc(s_xT, 1)

            def project(k):
                if k == 0:
                    pe.wait_ge(s_wc, 3)
                for h in range(2):
                    pe.wait_ge(s_cpT, 2 * k + h + 1)
                    for c in range(C):
                        done = nc.tensor.matmul(projection_of(k, h)[:, P * c:P * c + P], xsT[h][:, P * c:P * c + P],
                                                wcT[:, :], start=True, stop=True)
                    done.then_inc(s_z, 1)

            transpose_x(0)
            project(0)

            def by_block(part):
                return part[:, :, :].rearrange("p (j c) n -> p j (c n)", c=C)

            def cosines(t):
                k = place_of(t)
                if k is not None and k < FAR:
                    pe.wait_ge(s_cpT, 2 * k + 2)
                    pe.wait_ge(s_loV, k + 2)
                    if k >= 1:
                        pe.wait_ge(s_loP, k)
                for c in range(C):
                    if k is not None and 2 <= k < FAR and c == 2:
                        pe.wait_ge(s_v, 2 * k + 2)
                    if last_place_of(t) is not None and last_place_of(t) >= 1 and c == 2:
                        pe.wait_ge(s_y, C * last_place_of(t))
                    if not (isinstance(t["g"], int) and t["g"] == 0) and c % 2 == 0:
                        pe.wait_ge(s_E, t["g"] * 2 - 1 + c // 2)
                    for n, (left, right) in enumerate(((xhi, xhi), (xhi, xlo), (xlo, xhi))):
                        done = nc.tensor.matmul(S[:, c, :], by_block(left)[:, t["J"], P * c:P * c + P],
                                                by_block(right)[:, t["I"], :],
                                                start=n == 0, stop=n == 2)
                    if c % 2:
                        done.then_inc(s_S, 1)

            def reads_v(p):
                return place_of(p) is not None or last_place_of(p) is not None

            def aggregate_d(p, chunks=range(C)):
                direct = reads_v(p)
                for c in chunks:
                    if c == 0:
                        if not direct:
                            pe.wait_ge(s_vJ[p["slot"]], (p["turn"] + 1) * 16)
                        if p["opens"] and not (isinstance(p["group"], int) and p["group"] == 0):
                            pe.wait_ge(s_addD, p["group"])
                        if place_of(p) == 0:
                            pe.wait_ge(s_v, 4)
                        pe.wait_ge(s_dmV, p["g"] * 2 + 2)
                    if c == C // 2:
                        pe.wait_ge(s_dmP, p["g"] * 2 + 2)
                    v_of_J = v[:, C * p["J"] + c, :] if direct else vJ[p["slot"]][:, c, :]
                    done = nc.tensor.matmul(accD[:, :], v_of_J, dT[p["slot"]][:, c, :],
                                            start=p["opens"] and c == 0, stop=p["closes"] and c == C - 1)
                if C - 1 in chunks:
                    done.then_inc(s_dagg, 1)

            def aggregate_x(p, h):
                direct = reads_v(p)
                if h == 0:
                    if not direct:
                        pe.wait_ge(s_vI, p["vI"] * 16)
                    if not isinstance(p["pairs"], int) or p["pairs"] > 1:
                        pe.wait_ge(s_addX, p["pairs"] - 1)
                    pe.wait_ge(s_xm, p["pairs"] * C)
                for c in range(2 * h, 2 * h + 2):
                    v_of_I = v[:, C * p["I"] + c, :] if direct else vI[:, c, :]
                    done = nc.tensor.matmul(accX[:, :], v_of_I, xT[p["slot"]][:, c, :],
                                            start=c == 0, stop=c == C - 1)
                if h == 1:
                    done.then_inc(s_xagg, 1)

            def transpose_E(t, h):
                chunks = (2 * h, 2 * h + 1)
                order = [(k, half) for half in range(2) for k in chunks] if h == 0 else \
                        [(k, half) for k in chunks for half in range(2)]
                if place_of(t) == 0 and h == 0:
                    pe.wait_ge(s_v, 2)
                    pe.wait_ge(s_const, 1)
                for k, half in order:
                    if h == 0 and k == 0:
                        pe.wait_ge(s_E, t["g"] * 2 + half + 1)
                    if half == 0 and not (h == 0 and isinstance(t["pairs"], int) and t["pairs"] == 1):
                        pe.wait_ge(s_xm, (t["pairs"] - 1) * C + k - 1)
                    for c in (2 * half, 2 * half + 1):
                        done = nc.tensor.transpose(ET[k % 2][:, P * c:P * c + P],
                                                   E[t["slot"]][:, c, P * k:P * k + P], ident[:, :])
                    if half == 1:
                        done.then_inc(s_ET, 1)

            def finish(n):
                J = FINAL[n]
                if n < EARLY:
                    pe.wait_ge(s_E, last[n]["g"] * 2 + 2)
                    pe.wait_ge(s_addX, FAR + NEAR * J)
                    pe.wait_ge(s_addD, FAR + J + 1)
                elif n < NB - 2:
                    pe.wait_ge(s_addX, last[n - EARLY + 1]["pairs"])
                elif n == NB - 2:
                    pe.wait_ge(s_addD, last[-1]["group"] + 1)
                if n >= EARLY + 1:
                    pe.wait_ge(s_y, C * max(n - 1, EARLY))
                for c in range(C):
                    m = C * J + c
                    if n == NB - 1:
                        pe.wait_ge(s_add_end, c + 1)
                    done = nc.tensor.matmul(final_of(n)[:, c // 2, c % 2, 0:D + 1], acc[:, P * m:P * m + P],
                                            restore[:, :], start=True, stop=True)
                done.then_inc(s_fT, 1)

            def step(t, p1, p2):
                cosines(t)
                if p1 is not None:
                    aggregate_d(p1, range(C) if p1["pair"] else range(C - 1))
                k = place_of(t)
                more = k is not None and k + 1 < FAR
                n = last_place_of(t)
                if k == 0:
                    transpose_x(1)
                for h in range(2):
                    if more and h == 1:
                        project(k + 1)
                    if n == 0 and h == 1:
                        finish(n)
                    if t["pair"]:
                        transpose_E(t, h)
                    if n is not None and n >= 1 and h == 0:
                        finish(n)
                    if more and h == 0 and k >= 1:
                        transpose_x(k + 1)
                    if p1 is not None and p1["pair"]:
                        aggregate_x(p1, h)
                    elif p1 is not None and h == 0:
                        aggregate_d(p1, range(C - 1, C))

            run(pe, step)
            finish(EARLY)
            aggregate_d(last[-1])
            finish(EARLY + 1)
            aggregate_x(last[-1], 0)
            aggregate_x(last[-1], 1)
            finish(EARLY + 2)
            finish(EARLY + 3)


def kernel(x, adj, L0_gnn_W, L0_gnn_bias, L0_gnn_b):
    import numpy as np
    import concourse.bacc as bacc
    from concourse.bass_utils import run_bass_kernel_spmd

    nc = bacc.Bacc("TRN2", target_bir_lowering=False, num_devices=1)
    arrays = dict(x=x, adj=adj, w=L0_gnn_W, bias=L0_gnn_bias, b=L0_gnn_b)
    arrays = {f"in_{k}": np.ascontiguousarray(a) for k, a in arrays.items()}
    ins = [nc.dram_tensor(k, a.shape, mybir.dt.from_np(a.dtype), kind="ExternalInput").ap() for k, a in arrays.items()]
    out = nc.dram_tensor("out", x.shape, mybir.dt.float32, kind="ExternalOutput").ap()
    adj_attention_layernorm(nc, *ins, out)
    return run_bass_kernel_spmd(nc, [arrays], core_ids=[0]).results[0]["out"]
```
